# Optimizing a Trainium2 kernel written in Bass

```python
import numpy as np
import jax
import jax.numpy as jnp

def _softmax(x, axis=-1):
    return jax.nn.softmax(x, axis=axis)

def _gelu(x):
    return jax.nn.gelu(x, approximate=True)

def _silu(x):
    return jax.nn.silu(x)

def _sigmoid(x):
    return jax.nn.sigmoid(x)

def _layernorm(x, axis=-1, eps=1e-05):
    m = jnp.mean(x, axis=axis, keepdims=True)
    v = jnp.var(x, axis=axis, keepdims=True)
    return (x - m) / jnp.sqrt(v + eps)

def _scatter_add(tgt, idx, src, axis=0):
    return tgt.at[idx].add(src)

def _segment_sum(src, seg, n):
    return jax.ops.segment_sum(src, seg, n)
kernel_name = 'mk_conv_seq_d4_conv_nchw512_r4_ee6c19'

def setup_inputs(seed: int=0):
    np.random.seed(seed)
    _w = jnp.asarray

    def _rec_inputs():
        import jax
        import jax.numpy as jnp
        _gk = jax.random.key(seed)
        x = 7.22e-05 + 1 * jax.random.normal(jax.random.fold_in(_gk, 1), (16, 128, 32, 32), jnp.float32)
        return x
    x = _rec_inputs()

    def _L0_conv_setup():
        import jax, jax.numpy as jnp
        import numpy as np
        C = 128
        HEADS = 8
        SCALE = C ** (-0.5)
        key = jax.random.key(seed)
        k0, k1, k2, k3, k4 = jax.random.split(key, 5)
        B, H, W = (16, 32, 32)
        x = jax.random.normal(k0, (B, C, H, W), dtype=jnp.float32)
        qkv_w = jax.random.normal(k1, (3 * C, C), dtype=jnp.float32) * C ** (-0.5)
        qkv_b = jax.random.normal(k2, (3 * C,), dtype=jnp.float32) * 0.01
        proj_w = jax.random.normal(k3, (C, C), dtype=jnp.float32) * C ** (-0.5)
        proj_b = jax.random.normal(k4, (C,), dtype=jnp.float32) * 0.01
        return {'x': x, 'qkv_w': qkv_w, 'qkv_b': qkv_b, 'proj_w': proj_w, 'proj_b': proj_b}
    _L0_conv_all = _L0_conv_setup()
    _L0_conv_in = {k: v for k, v in _L0_conv_all.items() if k in ('qkv_w', 'qkv_b', 'proj_w', 'proj_b')}
    del _L0_conv_all

    def _L1_conv_setup():
        import jax, jax.numpy as jnp
        import numpy as np
        GROUPS = 8
        EPS = 0.01

        def _group_stats(x, G, eps):
            N, C, H, W = x.shape
            M = N * H * W
            Cg = C // G
            xf = jnp.transpose(x, (1, 0, 2, 3)).reshape(C, M)
            mu = jnp.mean(xf, axis=1, keepdims=True)
            xc = xf - mu
            xg = xc.reshape(G, Cg, M)
            cov = jnp.einsum('gim,gjm->gij', xg, xg) / M + eps * jnp.eye(Cg, dtype=x.dtype)
            return (xg, cov, mu)
        key = jax.random.key(seed)
        k1, k2 = jax.random.split(key)
        N, C, H, W = (4, 128, 32, 32)
        c_A = jax.random.normal(k1, (N, C, H, W), dtype=jnp.float32)
        s_B = jax.random.normal(k2, (N, C, H, W), dtype=jnp.float32)
        return {'c_A': c_A, 's_B': s_B}
    _L1_conv_all = _L1_conv_setup()
    _L1_conv_in = {k: v for k, v in _L1_conv_all.items() if k in ('s_B',)}
    del _L1_conv_all

    def _L2_conv_setup():
        import jax, jax.numpy as jnp
        import numpy as np
        import math
        B, C, H, W = (8, 128, 32, 32)
        NH = 8
        G = 32
        EPS = 1e-06

        def group_norm(x, gamma, beta, groups=G, eps=EPS):
            b, c, h, w = x.shape
            xr = x.reshape(b, groups, c // groups, h, w)
            mu = xr.mean(axis=(2, 3, 4), keepdims=True)
            var = xr.var(axis=(2, 3, 4), keepdims=True)
            xn = ((xr - mu) * jax.lax.rsqrt(var + eps)).reshape(b, c, h, w)
            return xn * gamma[None, :, None, None] + beta[None, :, None, None]

        def conv2d(x, w, b, pad):
            y = jax.lax.conv_general_dilated(x, w, window_strides=(1, 1), padding=[(pad, pad), (pad, pad)], dimension_numbers=('NCHW', 'OIHW', 'NCHW'))
            return y + b[None, :, None, None]
        key = jax.random.key(seed)
        ks = jax.random.split(key, 20)

        def n(k, shape, s=0.02):
            return jax.random.normal(k, shape, dtype=jnp.float32) * s
        f32 = jnp.float32
        return {'hidden_states': jax.random.normal(ks[0], (B, C, H, W), dtype=f32), 'pre_g': jnp.ones(C, f32), 'pre_b': jnp.zeros(C, f32), 'norm_g': jnp.ones(C, f32), 'norm_b': jnp.zeros(C, f32), 'post_g': jnp.ones(C, f32), 'post_b': jnp.zeros(C, f32), 'pos_emb': n(ks[1], (1, C, 32, 32)), 'wq': n(ks[2], (C, C)), 'wk': n(ks[3], (C, C)), 'wv': n(ks[4], (C, C)), 'wq0': n(ks[5], (C // 2, C)), 'wq1': n(ks[6], (C // 2, C)), 'wk0': n(ks[7], (C // 2, C)), 'wk1': n(ks[8], (C // 2, C)), 'wv0': n(ks[9], (C // 2, C)), 'wv1': n(ks[10], (C // 2, C)), 'sa_w1': n(ks[11], (C // 8, C, 1, 1)), 'sa_b1': jnp.zeros(C // 8, f32), 'sa_w2': n(ks[12], (C // 8, C // 8, 3, 3)), 'sa_b2': jnp.zeros(C // 8, f32), 'sa_w3': n(ks[13], (1, C // 8, 1, 1)), 'sa_b3': jnp.zeros(1, f32), 'ff_w1': n(ks[14], (C, 2 * C)), 'ff_b1': jnp.zeros(C, f32), 'ff_w2': n(ks[15], (C, C)), 'ff_b2': jnp.zeros(C, f32), 'out_w': n(ks[16], (C, C)), 'out_b': jnp.zeros(C, f32)}
    _L2_conv_all = _L2_conv_setup()
    _L2_conv_in = {k: v for k, v in _L2_conv_all.items() if k in ('pre_g', 'pre_b', 'norm_g', 'norm_b', 'post_g', 'post_b', 'pos_emb', 'wq', 'wk', 'wv', 'wq0', 'wq1', 'wk0', 'wk1', 'wv0', 'wv1', 'sa_w1', 'sa_b1', 'sa_w2', 'sa_b2', 'sa_w3', 'sa_b3', 'ff_w1', 'ff_b1', 'ff_w2', 'ff_b2', 'out_w', 'out_b')}
    del _L2_conv_all

    def _L3_conv_setup():
        import jax, jax.numpy as jnp
        import numpy as np
        key = jax.random.key(seed)
        ks = jax.random.split(key, 8)
        B, C, H, W = (4, 128, 16, 16)
        C8 = C // 8
        return {'x': jax.random.normal(ks[0], (B, C, H, W), dtype=jnp.float32), 'Wq': jax.random.normal(ks[1], (C8, C), dtype=jnp.float32) * 0.02, 'bq': jax.random.normal(ks[2], (C8,), dtype=jnp.float32) * 0.02, 'Wk': jax.random.normal(ks[3], (C8, C), dtype=jnp.float32) * 0.02, 'bk': jax.random.normal(ks[4], (C8,), dtype=jnp.float32) * 0.02, 'Wv': jax.random.normal(ks[5], (C, C), dtype=jnp.float32) * 0.02, 'bv': jax.random.normal(ks[6], (C,), dtype=jnp.float32) * 0.02, 'gamma': jax.random.normal(ks[7], (1,), dtype=jnp.float32)}
    _L3_conv_all = _L3_conv_setup()
    _L3_conv_in = {k: v for k, v in _L3_conv_all.items() if k in ('Wq', 'bq', 'Wk', 'bk', 'Wv', 'bv', 'gamma')}
    del _L3_conv_all
    return {'x': x, 'L0_conv_qkv_w': _L0_conv_in['qkv_w'], 'L0_conv_qkv_b': _L0_conv_in['qkv_b'], 'L0_conv_proj_w': _L0_conv_in['proj_w'], 'L0_conv_proj_b': _L0_conv_in['proj_b'], 'L1_conv_s_B': _L1_conv_in['s_B'], 'L2_conv_pre_g': _L2_conv_in['pre_g'], 'L2_conv_pre_b': _L2_conv_in['pre_b'], 'L2_conv_norm_g': _L2_conv_in['norm_g'], 'L2_conv_norm_b': _L2_conv_in['norm_b'], 'L2_conv_post_g': _L2_conv_in['post_g'], 'L2_conv_post_b': _L2_conv_in['post_b'], 'L2_conv_pos_emb': _L2_conv_in['pos_emb'], 'L2_conv_wq': _L2_conv_in['wq'], 'L2_conv_wk': _L2_conv_in['wk'], 'L2_conv_wv': _L2_conv_in['wv'], 'L2_conv_wq0': _L2_conv_in['wq0'], 'L2_conv_wq1': _L2_conv_in['wq1'], 'L2_conv_wk0': _L2_conv_in['wk0'], 'L2_conv_wk1': _L2_conv_in['wk1'], 'L2_conv_wv0': _L2_conv_in['wv0'], 'L2_conv_wv1': _L2_conv_in['wv1'], 'L2_conv_sa_w1': _L2_conv_in['sa_w1'], 'L2_conv_sa_b1': _L2_conv_in['sa_b1'], 'L2_conv_sa_w2': _L2_conv_in['sa_w2'], 'L2_conv_sa_b2': _L2_conv_in['sa_b2'], 'L2_conv_sa_w3': _L2_conv_in['sa_w3'], 'L2_conv_sa_b3': _L2_conv_in['sa_b3'], 'L2_conv_ff_w1': _L2_conv_in['ff_w1'], 'L2_conv_ff_b1': _L2_conv_in['ff_b1'], 'L2_conv_ff_w2': _L2_conv_in['ff_w2'], 'L2_conv_ff_b2': _L2_conv_in['ff_b2'], 'L2_conv_out_w': _L2_conv_in['out_w'], 'L2_conv_out_b': _L2_conv_in['out_b'], 'L3_conv_Wq': _L3_conv_in['Wq'], 'L3_conv_bq': _L3_conv_in['bq'], 'L3_conv_Wk': _L3_conv_in['Wk'], 'L3_conv_bk': _L3_conv_in['bk'], 'L3_conv_Wv': _L3_conv_in['Wv'], 'L3_conv_bv': _L3_conv_in['bv'], 'L3_conv_gamma': _L3_conv_in['gamma']}

def reference(x, L0_conv_qkv_w, L0_conv_qkv_b, L0_conv_proj_w, L0_conv_proj_b, L1_conv_s_B, L2_conv_pre_g, L2_conv_pre_b, L2_conv_norm_g, L2_conv_norm_b, L2_conv_post_g, L2_conv_post_b, L2_conv_pos_emb, L2_conv_wq, L2_conv_wk, L2_conv_wv, L2_conv_wq0, L2_conv_wq1, L2_conv_wk0, L2_conv_wk1, L2_conv_wv0, L2_conv_wv1, L2_conv_sa_w1, L2_conv_sa_b1, L2_conv_sa_w2, L2_conv_sa_b2, L2_conv_sa_w3, L2_conv_sa_b3, L2_conv_ff_w1, L2_conv_ff_b1, L2_conv_ff_w2, L2_conv_ff_b2, L2_conv_out_w, L2_conv_out_b, L3_conv_Wq, L3_conv_bq, L3_conv_Wk, L3_conv_bk, L3_conv_Wv, L3_conv_bv, L3_conv_gamma):
    import jax
    import jax.numpy as jnp

    def _L0_conv_ref(x, qkv_w, qkv_b, proj_w, proj_b):
        import jax, jax.numpy as jnp
        import numpy as np
        C = 128
        HEADS = 8
        SCALE = C ** (-0.5)
        b, c, h, w = x.shape
        n = h * w
        hd = c // HEADS
        qkv = jnp.einsum('oc,bchw->bohw', qkv_w, x) + qkv_b[None, :, None, None]
        q, k, v = jnp.split(qkv, 3, axis=1)
        q = q.reshape(b, HEADS, hd, n)
        k = k.reshape(b, HEADS, hd, n)
        v = v.reshape(b, HEADS, hd, n)
        attn = jnp.einsum('bhcn,bhcm->bhnm', q, k) * SCALE
        attn = jax.nn.softmax(attn, axis=-1)
        out = jnp.einsum('bhnm,bhcm->bhcn', attn, v)
        out = out.reshape(b, c, h, w)
        out = jnp.einsum('oc,bchw->bohw', proj_w, out) + proj_b[None, :, None, None]
        return x + out

    def _L1_conv_ref(c_A, s_B):
        import jax, jax.numpy as jnp
        import numpy as np
        GROUPS = 8
        EPS = 0.01

        def _group_stats(x, G, eps):
            N, C, H, W = x.shape
            M = N * H * W
            Cg = C // G
            xf = jnp.transpose(x, (1, 0, 2, 3)).reshape(C, M)
            mu = jnp.mean(xf, axis=1, keepdims=True)
            xc = xf - mu
            xg = xc.reshape(G, Cg, M)
            cov = jnp.einsum('gim,gjm->gij', xg, xg) / M + eps * jnp.eye(Cg, dtype=x.dtype)
            return (xg, cov, mu)
        N, C, H, W = c_A.shape
        G, eps = (GROUPS, EPS)
        M = N * H * W
        cg, c_cov, c_mu = _group_stats(c_A, G, eps)
        sg, s_cov, s_mu = _group_stats(s_B, G, eps)
        c_e, c_v = jnp.linalg.eigh(c_cov)
        s_e, s_v = jnp.linalg.eigh(s_cov)
        whitening = jnp.einsum('gik,gk,gjk->gij', c_v, c_e ** (-0.5), c_v)
        coloring = jnp.einsum('gik,gk,gjk->gij', s_v, s_e ** 0.5, s_v)
        colored = jnp.einsum('gij,gjk,gkm->gim', coloring, whitening, cg)
        styleized = colored.reshape(C, M) + s_mu
        return jnp.transpose(styleized.reshape(C, N, H, W), (1, 0, 2, 3))

    def _L2_conv_ref(hidden_states, pre_g, pre_b, norm_g, norm_b, post_g, post_b, pos_emb, wq, wk, wv, wq0, wq1, wk0, wk1, wv0, wv1, sa_w1, sa_b1, sa_w2, sa_b2, sa_w3, sa_b3, ff_w1, ff_b1, ff_w2, ff_b2, out_w, out_b):
        import jax, jax.numpy as jnp
        import numpy as np
        import math
        B, C, H, W = (8, 128, 32, 32)
        NH = 8
        G = 32
        EPS = 1e-06

        def group_norm(x, gamma, beta, groups=G, eps=EPS):
            b, c, h, w = x.shape
            xr = x.reshape(b, groups, c // groups, h, w)
            mu = xr.mean(axis=(2, 3, 4), keepdims=True)
            var = xr.var(axis=(2, 3, 4), keepdims=True)
            xn = ((xr - mu) * jax.lax.rsqrt(var + eps)).reshape(b, c, h, w)
            return xn * gamma[None, :, None, None] + beta[None, :, None, None]

        def conv2d(x, w, b, pad):
            y = jax.lax.conv_general_dilated(x, w, window_strides=(1, 1), padding=[(pad, pad), (pad, pad)], dimension_numbers=('NCHW', 'OIHW', 'NCHW'))
            return y + b[None, :, None, None]
        b, c, h, w = hidden_states.shape
        S = h * w
        residual = hidden_states
        x = group_norm(hidden_states, pre_g, pre_b)
        x = x + pos_emb
        s1 = jax.nn.silu(conv2d(x, sa_w1, sa_b1, 0))
        s2 = jax.nn.silu(conv2d(s1, sa_w2, sa_b2, 1))
        spatial_weights = jax.nn.sigmoid(conv2d(s2, sa_w3, sa_b3, 0))
        spatial_enhanced = x * spatial_weights
        sh = group_norm(x, norm_g, norm_b).reshape(b, c, S).transpose(0, 2, 1)
        enc = sh
        hd = c // NH

        def split_heads(t):
            return t.reshape(b, S, NH, hd).transpose(0, 2, 1, 3)
        qh = split_heads(sh @ wq.T)
        kh = split_heads(enc @ wk.T)
        vh = split_heads(enc @ wv.T)
        scores = jnp.einsum('bhqd,bhkd->bhqk', qh, kh) / math.sqrt(hd)
        probs = jax.nn.softmax(scores, axis=-1)
        standard_out = jnp.einsum('bhqk,bhkd->bhqd', probs, vh)
        standard_out = standard_out.transpose(0, 2, 1, 3).reshape(b, S, c)
        msh = spatial_enhanced.reshape(b, c, S).transpose(0, 2, 1)
        parts = []
        for wqm, wkm, wvm in ((wq0, wk0, wv0), (wq1, wk1, wv1)):
            qm = msh @ wqm.T
            km = enc @ wkm.T
            vm = enc @ wvm.T
            sc = jnp.einsum('bqd,bkd->bqk', qm, km) / math.sqrt(qm.shape[-1])
            parts.append(jnp.einsum('bqk,bkd->bqd', jax.nn.softmax(sc, axis=-1), vm))
        multi_out = jnp.concatenate(parts, axis=-1)
        combined = jnp.concatenate([standard_out, multi_out], axis=-1)
        fused = jax.nn.silu(combined @ ff_w1.T + ff_b1) @ ff_w2.T + ff_b2
        final = fused @ out_w.T + out_b
        final = final.transpose(0, 2, 1).reshape(b, c, h, w)
        final = group_norm(final, post_g, post_b)
        return final + residual

    def _L3_conv_ref(x, Wq, bq, Wk, bk, Wv, bv, gamma):
        import jax, jax.numpy as jnp
        import numpy as np
        B, C, H, W = x.shape
        N = H * W
        xf = x.reshape(B, C, N)
        q = jnp.einsum('oc,bcn->bno', Wq, xf) + bq
        k = jnp.einsum('oc,bcn->bon', Wk, xf) + bk[None, :, None]
        v = jnp.einsum('oc,bcn->bon', Wv, xf) + bv[None, :, None]
        energy = jnp.einsum('bno,bom->bnm', q, k)
        attention = jax.nn.softmax(energy, axis=-1)
        out = jnp.einsum('bcm,bnm->bcn', v, attention).reshape(B, C, H, W)
        return gamma[0] * out + x

    def _gn(v, G=32, eps=1e-05):
        B_, C_, H_, W_ = v.shape
        g = v.reshape(B_, G, C_ // G, H_, W_)
        m = jnp.mean(g, axis=(2, 3, 4), keepdims=True)
        s = jnp.var(g, axis=(2, 3, 4), keepdims=True)
        return ((g - m) / jnp.sqrt(s + eps)).reshape(v.shape)

    def _ln_c(v, eps=1e-06):
        m = jnp.mean(v, axis=1, keepdims=True)
        s = jnp.var(v, axis=1, keepdims=True)
        return (v - m) / jnp.sqrt(s + eps)

    def _ln_t(v, eps=1e-05):
        m = jnp.mean(v, axis=-1, keepdims=True)
        s = jnp.var(v, axis=-1, keepdims=True)
        return (v - m) / jnp.sqrt(s + eps)

    def _to_tokens(v):
        B_, C_, H_, W_ = v.shape
        return v.reshape(B_, C_, H_ * W_).transpose(0, 2, 1)

    def _from_tokens(t, like):
        B_, C_, H_, W_ = like.shape
        return t.transpose(0, 2, 1).reshape(B_, C_, H_, W_)
    x = _L0_conv_ref(x, L0_conv_qkv_w, L0_conv_qkv_b, L0_conv_proj_w, L0_conv_proj_b)
    x = _L1_conv_ref(x, L1_conv_s_B)
    x = _L2_conv_ref(x, L2_conv_pre_g, L2_conv_pre_b, L2_conv_norm_g, L2_conv_norm_b, L2_conv_post_g, L2_conv_post_b, L2_conv_pos_emb, L2_conv_wq, L2_conv_wk, L2_conv_wv, L2_conv_wq0, L2_conv_wq1, L2_conv_wk0, L2_conv_wk1, L2_conv_wv0, L2_conv_wv1, L2_conv_sa_w1, L2_conv_sa_b1, L2_conv_sa_w2, L2_conv_sa_b2, L2_conv_sa_w3, L2_conv_sa_b3, L2_conv_ff_w1, L2_conv_ff_b1, L2_conv_ff_w2, L2_conv_ff_b2, L2_conv_out_w, L2_conv_out_b)
    x = _L3_conv_ref(x, L3_conv_Wq, L3_conv_bq, L3_conv_Wk, L3_conv_bk, L3_conv_Wv, L3_conv_bv, L3_conv_gamma)
    return x

_drawn_inputs = setup_inputs


def setup_inputs(seed=0):
    import zlib

    import numpy as np

    out = dict(_drawn_inputs(seed))
    spreads = {'L2_conv_pre_g': (1.0, 0.6),
     'L2_conv_pre_b': (0.0, 0.8),
     'L2_conv_norm_g': (1.0, 0.6),
     'L2_conv_norm_b': (0.0, 0.8),
     'L2_conv_post_g': (1.0, 0.2),
     'L2_conv_post_b': (0.0, 0.1),
     'L2_conv_sa_b1': (0.0, 0.8),
     'L2_conv_sa_b2': (0.0, 2.0),
     'L2_conv_ff_b1': (0.0, 0.381),
     'L2_conv_ff_b2': (0.0, 0.1),
     'L2_conv_out_b': (0.0, 0.1)}
    factors = {'L0_conv_qkv_b': 200.0,
     'L0_conv_proj_b': 200.0,
     'L2_conv_pos_emb': 8.0,
     'L2_conv_wq': 8.0,
     'L2_conv_wk': 8.0,
     'L2_conv_wv': 8.0,
     'L2_conv_wq0': 8.0,
     'L2_conv_wq1': 8.0,
     'L2_conv_wk0': 8.0,
     'L2_conv_wk1': 8.0,
     'L2_conv_wv0': 8.0,
     'L2_conv_wv1': 8.0,
     'L2_conv_sa_w1': 8.0,
     'L2_conv_sa_w2': 8.0,
     'L2_conv_sa_w3': 8.0,
     'L2_conv_ff_w1': 8.0,
     'L3_conv_Wq': 8.0,
     'L3_conv_bq': 27.318,
     'L3_conv_Wk': 8.0,
     'L3_conv_bk': 200.0,
     'L3_conv_Wv': 5.719,
     'L3_conv_bv': 60.731}
    for name, (base, spread) in spreads.items():
        noise = np.random.default_rng([zlib.crc32(name.encode()), seed]).standard_normal(out[name].shape)
        drawn = base * np.exp(spread * noise) if base else spread * noise
        out[name] = jnp.asarray(drawn.astype(out[name].dtype))
    for name, factor in factors.items():
        out[name] = (out[name] * factor).astype(out[name].dtype)
    return out
```

```python
from contextlib import ExitStack

import numpy as np

import concourse.bass as bass
from concourse import mybir

F32, BF16 = mybir.dt.float32, mybir.dt.bfloat16
ACT, ALU, AX = mybir.ActivationFunctionType, mybir.AluOpType, mybir.AxisListType

P = 128
NB = 16
SIDE = 32
N = SIDE * SIDE
KC = N // P
HEADS, HD = 8, P // 8
STYLES = 4
CG = 16
EPS_COV, EPS_GN = 0.01, 1e-6
ROOT_STEPS = 30
TERMS = [(0, 0), (0, 1), (1, 0), (0, 2), (2, 0), (1, 1)]
SROWS = 16 * len(TERMS) + 2


class Batch:

    def __init__(self, k, p):
        self.k, self.p = k, p

    def plus(self, n):
        return Batch(self.k, self.p + n)

    def times(self, n, c=0):
        return self.k * (2 * n) + (n * self.p + c)

    def pairs(self, n):
        return self.k * n + (self.p // 2 + 1) * n

    @property
    def parity(self):
        return self.p % 2

    def index(self):
        return (self.k * 2 + self.p) % NB


def ready_values(eng, *values):
    return [v if isinstance(v, int) else eng.snap(v) for v in values]


def some(value):
    return not (isinstance(value, int) and value <= 0)


class Group:

    def __init__(self, kind, heads, first, width):
        self.kind, self.heads, self.first, self.width = kind, heads, first, width


class Plan:

    def __init__(self, groups, proj):
        self.groups, self.proj = groups, proj
        self.s_groups = [g for g, x in enumerate(groups) if x.kind == "S"]
        self.d_group = next((g for g, x in enumerate(groups) if x.kind == "D"), None)
        self.mixed = bool(self.s_groups) and self.d_group is not None
        self.units = sum(g.heads * KC for g in groups)
        self.quads = KC * len(groups)
        self.maxes = sum(g.heads * KC * 2 for g in groups)
        self.d_heads = groups[self.d_group].heads if self.d_group is not None else 0
        self.prologue = self.load_steps(0) + self.max_steps(0, 0) + [("turn", 0, 0)] + self.scores(0, 0, 0)
        self.first = self.image(False, True)
        self.usual = self.image(True, True)
        self.last = self.image(True, False)
        self.epilogue = self.tail(0)

    def qk_steps(self, b):
        return [("qk", b, t) for t in range(4)] + [("split", b), ("stack", b)]

    def dqk_steps(self, b):
        return [("dqk", b, w, h, half) for w in range(2) for h in range(self.d_heads) for half in range(2)]

    def v_steps(self, b):
        s = [("v", b, t) for t in range(2)] if self.s_groups else []
        return s + ([("vd", b, t) for t in range(2)] if self.d_heads else [])

    def load_steps(self, b):
        if self.mixed:
            return [("load", b)] + self.qk_steps(b) + self.v_steps(b)
        return [("load", b)] + (self.qk_steps(b) if self.s_groups else self.dqk_steps(b)) + self.v_steps(b) + [("load", b + 1)]

    def make_steps(self, g, ahead):
        last = g == len(self.groups) - 1
        out = []
        if self.mixed and g == 0:
            out += self.dqk_steps(0) + [("load", 1)]
        if ahead and g == (1 if self.mixed else 0):
            out += self.qk_steps(1) if self.s_groups else self.dqk_steps(1)
        if ahead and last:
            out += self.v_steps(1) + ([] if self.mixed else [("load", 2)])
        return out

    def max_steps(self, b, g):
        return [("max", b, g, h, qc, half) for h in range(self.groups[g].heads) for qc in range(KC) for half in range(2)]

    def tail(self, b):
        g = len(self.groups) - 1
        return [("norm", b, g, 0), ("norm", b, g, 1), ("scale", b, g, 0), ("scale", b, g, 1)] + self.finish(b)

    def with_norms(self, b, g, maxes):
        norm = [("norm", b, g, half) for half in range(2)]
        scale = [("scale", b, g, half) for half in range(2)]
        return maxes[:4] + norm[:1] + maxes[4:5] + norm[1:] + maxes[5:9] + scale[:1] + maxes[9:11] + scale[1:] + maxes[11:]

    def finish(self, b):
        return [("proj", b, 0), ("proj", b, 1), ("store", b), ("residual", b + 1)]

    def scores(self, b, g, kc):
        return [("scores", b, g, kc, h) for h in range(self.groups[g].heads)]

    def image(self, tail, ahead):
        out = []
        n = len(self.groups)
        for g in range(n):
            last = g == n - 1
            nb, ng = (1, 0) if last else (0, g + 1)
            maxes = self.max_steps(nb, ng) if (ahead or not last) else []
            if g > 0:
                maxes = self.with_norms(0, g - 1, maxes)
            elif tail:
                maxes = self.with_norms(-1, n - 1, maxes)
                cut = min(len(maxes), 26)
                maxes = maxes[:cut] + self.finish(-1) + maxes[cut:]
            work = self.make_steps(g, ahead) + maxes
            turn = [("turn", nb, ng)] if (ahead or not last) else []
            gaps = 4 * (KC - 1)
            share = [work[len(work) * i // gaps:len(work) * (i + 1) // gaps] for i in range(gaps)]
            for kc in range(KC):
                pv = [("pv", 0, g, kc, half) for half in range(2)]
                if kc < KC - 1:
                    nxt = self.scores(0, g, kc + 1)
                    four = [nxt[:1], nxt[1:2], nxt[2:3], nxt[3:]]
                    a = share[4 * kc:4 * kc + 4]
                    out += four[0] + a[0] + four[1] + pv[:1] + a[1] + four[2] + pv[1:] + a[2] + four[3] + a[3]
                else:
                    nxt = self.scores(nb, ng, 0) if (ahead or not last) else []
                    out += turn + pv + [("evacuate", 0, g)] + nxt
        return out

    BANKED = ("qk", "dqk", "v", "vd", "max", "turn", "norm", "proj")

    def banked(self, steps):
        return [s for s in steps if self.is_banked(s)]

    def is_banked(self, step):
        return step[0] in self.BANKED and (self.proj or step[0] != "proj")

    def bank_of(self, section, i):
        pro, first, usual = (len(self.banked(x)) for x in (self.prologue, self.first, self.usual))
        where, p = section
        if where == "prologue":
            n, slope = i, 0
        elif where == "epilogue":
            n, slope = pro + first + (NB - 2) * usual + len(self.banked(self.last)) + i, 0
        elif where == "loop":
            n, slope = pro + first + (p - 1) * usual + i, usual
        else:
            n, slope = (pro + i if p == 0 else pro + first + (p - 1) * usual + i), 0
        return n % 2, slope, n // 2 + 1

    def unit(self, g, kc, h):
        return sum(x.heads * KC for x in self.groups[:g]) + kc * self.groups[g].heads + h

    def quad(self, g, kc):
        return g * KC + kc

    def max_number(self, g, h, qc, half):
        return sum(x.heads * KC * 2 for x in self.groups[:g]) + (h * KC + qc) * 2 + half


def walk(eng, plan, do):

    def section(steps, image, where):
        n = 0
        for step in steps:
            bank = None
            if plan.is_banked(step):
                at, slope, const = plan.bank_of(where, n)
                bank = (at, image.k * slope + const if slope else const)
                n += 1
            do(step, image, bank)

    section(plan.prologue, Batch(0, 0), ("prologue", 0))
    section(plan.first, Batch(0, 0), ("peeled", 0))
    section(plan.usual, Batch(0, 1), ("peeled", 1))
    with eng.Fori(1, NB // 2 - 1) as k:
        section(plan.usual, Batch(k, 0), ("loop", 0))
        section(plan.usual, Batch(k, 1), ("loop", 1))
    section(plan.usual, Batch(NB // 2 - 1, 0), ("peeled", NB - 2))
    section(plan.last, Batch(NB // 2 - 1, 1), ("peeled", NB - 1))
    section(plan.epilogue, Batch(NB // 2 - 1, 1), ("epilogue", 0))


def attention(nc, tag, plan, shared, W, x_in, xe_in, res_in, out, scratch, scale_q, bias, final):
    G = plan.groups
    zero, ident, ones, spread = (shared[n] for n in ("zero", "ident", "ones", "spread"))
    S = bool(plan.s_groups)
    D = plan.d_heads
    VW = G[plan.d_group].width if D else 0
    with ExitStack() as ctx:
        sb = lambda name, shape, dt: ctx.enter_context(nc.sbuf_tensor(f"{tag}_{name}", shape, dt))
        sem = lambda name: nc.alloc_semaphore(f"{tag}_{name}")
        pairs = shared["bank_pairs"]
        st = [pairs[i].rearrange("p a b -> p (a b)") for i in range(2)]
        po = pairs[2]
        bk = [pairs[3][:, i, :] for i in range(2)]

        xin = sb("xin", [P, N], F32)
        xe = sb("xe", [P, N], F32) if xe_in is not None else xin
        if S:
            qkf = sb("qkf", [P, 2, N], F32)
            parts = [sb(f"parts{w}", [P, 3, N], BF16) for w in range(2)]
            stack = [[sb(f"stack{w}{p}", [SROWS, 8, N], BF16) for p in range(2)] for w in range(2)]
            vs = [sb(f"vs{p}", [P, KC, 8, 32], F32) for p in range(2)]
            top = sb("top", [P, P], BF16)
            low = sb("low", [P, P], BF16)
        if D:
            dq = [[sb(f"dqk{w}{p}", [65, D, N], F32) for p in range(1 if S else 2)] * (2 if S else 1) for w in range(2)]
            vd = [sb(f"vd{p}", [P, KC, P], F32) for p in range(2)]
            esum = [sb(f"esum{p}", [P, D, N], F32) for p in range(1 if S else 2)] * (2 if S else 1)
            turned = sb("turned", [P, P], F32)
        ring = max(g.heads for g in G)
        e = [sb(f"e{i}", [P, ring, N], F32) for i in range(2)]
        osb = [sb(f"osb{g}", [P, N], F32) for g in range(len(G))]
        r = sb("r", [P, 2, 512], F32)
        y = sb("y", [P, N], F32)
        res = sb("res", [P, N], F32) if res_in is not None else None
        mx = sb("mx", [P, ring * KC, 2], F32)
        negm = sb("negm", [P, P], F32)

        const_ready = sem("const_ready")
        x_loaded = sem("x_loaded")
        res_loaded = sem("res_loaded")
        qk_evacuated = sem("qk_evacuated")
        split_step = sem("split_step")
        q_split = sem("q_split")
        parts_stored = sem("parts_stored")
        stack_ready = sem("stack_ready")
        dqk_ready = sem("dqk_ready")
        v_ready = sem("v_ready")
        max_done = sem("max_done")
        negmax_ready = sem("negmax_ready")
        top_ready = sem("top_ready")
        turned_ready = sem("turned_ready")
        smax_ready = sem("smax_ready")
        dmax_ready = sem("dmax_ready")
        scores_ready = sem("scores_ready")
        exp_done = sem("exp_done")
        esum_done = sem("esum_done")
        pv_done = sem("pv_done")
        out_ready = sem("out_ready")
        evacuated = sem("evacuated")
        bank_full = [sem(f"bank_full{i}") for i in range(2)]
        bank_free = [sem(f"bank_free{i}") for i in range(2)]
        ln_done = sem("ln_done")
        recip_ready = sem("recip_ready")
        norm_done = sem("norm_done")
        y_step = sem("y_step")
        y_ready = sem("y_ready")
        stored = sem("stored")
        block = ctx.enter_context(nc.Block())

        n_g = len(G)
        n_norm = 2 * n_g
        n_vs = 2 * S + 2 * bool(D)
        n_loads = 2 if xe_in is not None else 1
        n_dqk = 4 * D
        n_const = (6 if S else 0) + ((1 if S else 2) if D else 0) + 1

        def skip(b):
            return isinstance(b.k, int) and 2 * b.k + b.p >= NB

        def since(image, rel):
            return not (isinstance(image.k, int) and 2 * image.k + image.p + rel < 0)

        @block.sync
        def _(sp):
            def do(step, image, bank):
                kind, b = step[0], image.plus(step[1])
                if kind in ("load", "residual", "store") and not isinstance(b.k, int):
                    row = sp.snap(b.index())
                else:
                    row = b.index()
                if kind == "load":
                    if skip(b):
                        return
                    if since(b, -1) and plan.mixed:
                        sp.wait_ge(dqk_ready, b.times(n_dqk))
                    elif since(b, -1):
                        sp.wait_ge(v_ready, b.times(n_vs))
                    sp.dma_start(xin[:, :], x_in[row]).then_inc(x_loaded, 16)
                    if xe_in is not None:
                        sp.dma_start(xe[:, :], xe_in[row]).then_inc(x_loaded, 16)
                if kind == "residual" and res is not None and not skip(b):
                    if since(b, -1):
                        sp.wait_ge(y_ready, b.times(2))
                    sp.dma_start(res[:, :], res_in[row]).then_inc(res_loaded, 16)
                if kind == "stack":
                    for w in range(2):
                        sp.wait_ge(q_split, b.times(2, 1 + w))
                        sp.dma_start(scratch[w].rearrange("t p n -> p t n"), parts[w][:, :, :]).then_inc(parts_stored, 16)
                    sp.wait_ge(parts_stored, b.times(32, 32))
                    for w in range(2):
                        for t in range(6):
                            src = scratch[w][TERMS[t][w]].rearrange("(h d) n -> d h n", d=16)
                            sp.dma_start(stack[w][b.parity][16 * t:16 * t + 16, :, :], src).then_inc(stack_ready, 16)
                if kind == "turn":
                    g = step[2]
                    sp.wait_ge(turned_ready, b.times(n_g, g + 1))
                    h0, rows = G[g].first, G[g].heads * KC
                    if G[g].kind == "S":
                        for row, part in ((96, top), (97, low)):
                            sp.dma_start(stack[0][b.parity][row:row + 1, h0:h0 + G[g].heads, :],
                                         part[0:rows, :]).then_inc(smax_ready, 16)
                    else:
                        sp.dma_start(dq[0][b.parity][64:65, :, :], turned[0:rows, :]).then_inc(dmax_ready, 16)
                if kind == "store":
                    sp.wait_ge(y_ready, b.times(2, 2))
                    sp.dma_start(out[row], y[:, :]).then_inc(stored, 16)

            if res is not None:
                sp.dma_start(res[:, :], res_in[0]).then_inc(res_loaded, 16)
            walk(sp, plan, do)
            sp.wait_ge(stored, 16 * NB)

        @block.gpsimd
        def _(pool):
            def do(step, image, bank):
                kind, b = step[0], image.plus(step[1])
                if kind == "split":
                    for w in range(2):
                        src, dst = qkf[:, w, :], parts[w]
                        nought = zero[:, 0:1].to_broadcast([P, N])
                        pool.wait_ge(qk_evacuated, b.times(4, 2 + 2 * w))
                        if since(b, -1):
                            pool.wait_ge(parts_stored, b.times(32))
                        nc.gpsimd.tensor_tensor(dst[:, 0, :], src, nought, ALU.add).then_inc(split_step, 1)
                        pool.wait_ge(split_step, b.times(6, 3 * w + 1))
                        nc.gpsimd.tensor_tensor(src, src, dst[:, 0, :], ALU.subtract).then_inc(split_step, 1)
                        pool.wait_ge(split_step, b.times(6, 3 * w + 2))
                        nc.gpsimd.tensor_tensor(dst[:, 1, :], src, nought, ALU.add).then_inc(split_step, 1)
                        pool.wait_ge(split_step, b.times(6, 3 * w + 3))
                        nc.gpsimd.tensor_tensor(dst[:, 2, :], src, dst[:, 1, :], ALU.subtract).then_inc(q_split, 1)
                if kind == "scores" and G[step[2]].kind == "D":
                    g, kc, h = step[2:]
                    pool.wait_ge(exp_done, b.times(plan.units, plan.unit(g, kc, h) + 1))
                    src = e[plan.quad(g, kc) % 2][:, h, :]
                    if kc == 0:
                        ago = 1 if S else 2
                        if since(b, -ago):
                            pool.wait_ge(ln_done, b.plus(1 - ago).times(n_norm))
                        nc.gpsimd.tensor_tensor(esum[b.parity][:, h, :], src, zero[:, 0:1].to_broadcast([P, N]), ALU.add).then_inc(esum_done, 1)
                    else:
                        pool.wait_ge(esum_done, b.times(KC * D, (kc - 1) * D + h + 1))
                        nc.gpsimd.tensor_tensor(esum[b.parity][:, h, :], src, esum[b.parity][:, h, :], ALU.add).then_inc(esum_done, 1)

            walk(pool, plan, do)

        @block.tensor
        def _(pe):
            half_of = lambda t, half: t[:, 512 * half:512 * half + 512]

            def do(step, image, bank):
                kind, b = step[0], image.plus(step[1])
                p = b.parity
                if bank is not None:
                    dst, full = bk[bank[0]], bank_full[bank[0]]
                    if not (isinstance(bank[1], int) and bank[1] < 2):
                        pe.wait_ge(bank_free[bank[0]], bank[1] - 1)
                if kind == "qk":
                    t = step[2]
                    if t == 0:
                        pe.wait_ge(x_loaded, b.times(16 * n_loads, 16 * n_loads))
                    nc.tensor.matmul(dst[:, :], W["qk"][t // 2], half_of(xin, t % 2), start=True, stop=True).then_inc(full, 1)
                if kind == "dqk":
                    w, h, half = step[2:]
                    if not S and (w, h, half) == (0, 0, 0):
                        pe.wait_ge(x_loaded, b.times(16 * n_loads, 16 * n_loads))
                    nc.tensor.matmul(dst[0:64, :], W["dqk"][w][h], half_of(xe if w == 0 else xin, half),
                                     start=True, stop=True).then_inc(full, 1)
                if kind in ("v", "vd"):
                    for c in range(4):
                        kc = 4 * step[2] + c
                        mm = nc.tensor.matmul(dst[:, P * c:P * c + P], xin[:, P * kc:P * kc + P], W[kind],
                                              start=True, stop=True)
                    mm.then_inc(full, 1)
                if kind == "max":
                    g, h, qc, half = step[2:]
                    if (h, qc, half) == (0, 0, 0):
                        if G[g].kind == "S":
                            pe.wait_ge(stack_ready, b.times(192, 192))
                        else:
                            pe.wait_ge(dqk_ready, b.times(n_dqk, n_dqk))
                    if G[g].kind == "S":
                        ah = G[g].first + h
                        lhs, rhs = stack[0][p][0:96, ah, P * qc:P * qc + P], stack[1][p][0:96, ah, 512 * half:512 * half + 512]
                    else:
                        lhs, rhs = dq[0][p][0:64, h, P * qc:P * qc + P], dq[1][p][0:64, h, 512 * half:512 * half + 512]
                    nc.tensor.matmul(dst[:, :], lhs, rhs, start=True, stop=True).then_inc(full, 1)
                if kind == "turn":
                    pe.wait_ge(negmax_ready, b.times(n_g, step[2] + 1))
                    nc.tensor.transpose(dst[:, 0:P], negm[:, :], ident[:, :]).then_inc(full, 1)
                if kind == "scores":
                    g, kc, h = step[2:]
                    u = plan.unit(g, kc, h)
                    if (kc, h) == (0, 0):
                        if G[g].kind == "S":
                            n_s = len(plan.s_groups)
                            pe.wait_ge(smax_ready, b.times(32 * n_s, 32 * (g + 1)))
                        else:
                            pe.wait_ge(dmax_ready, b.times(16, 16))
                            pe.wait_ge(const_ready, n_const)
                    if not (isinstance(b.k, int) and 2 * b.k + b.p == 0 and u < 2):
                        pe.wait_ge(exp_done, b.times(plan.units, u - 1))
                    for half in range(2):
                        if G[g].kind == "S":
                            ah = G[g].first + h
                            lhs, rhs = stack[1][p][:, ah, P * kc:P * kc + P], stack[0][p][:, ah, 512 * half:512 * half + 512]
                        else:
                            lhs, rhs = dq[1][p][:, h, P * kc:P * kc + P], dq[0][p][:, h, 512 * half:512 * half + 512]
                        mm = nc.tensor.matmul(st[u % 2][:, 512 * half:512 * half + 512], lhs, rhs, start=True, stop=True)
                    mm.then_inc(scores_ready, 1)
                if kind == "pv":
                    g, kc, half = step[2:]
                    if half == 0:
                        pe.wait_ge(exp_done, b.times(plan.units, plan.unit(g, kc, G[g].heads - 1) + 1))
                        if kc == 0:
                            if G[g].kind == "S" and g == 0 or not S:
                                pe.wait_ge(v_ready, b.times(n_vs, n_vs))
                            if g or since(b, -1):
                                pe.wait_ge(evacuated, b.times(n_g, g))
                    for h in range(G[g].heads):
                        src = e[plan.quad(g, kc) % 2][:, h, 512 * half:512 * half + 512]
                        width = G[g].width
                        v = vs[p][:, kc, G[g].first + h, :] if G[g].kind == "S" else vd[p][:, kc, width * h:width * h + width]
                        mm = nc.tensor.matmul(po[width * h:width * h + width, half, :], v, src,
                                              start=(kc == 0), stop=(kc == KC - 1), skip_group_check=True,
                                              tile_position=(0, width * h) if width < P else None)
                    if half == 1:
                        mm.then_inc(pv_done, 1)
                if kind == "norm":
                    g, half = step[2:]
                    pe.wait_ge(evacuated, b.times(n_g, g + 1))
                    if G[g].kind == "S":
                        mm = nc.tensor.matmul(dst[:, :], spread[:, :], half_of(osb[g], half), start=True, stop=True)
                    else:
                        pe.wait_ge(esum_done, b.times(KC * D, KC * D))
                        width = G[g].width
                        for h in range(D):
                            mm = nc.tensor.matmul(dst[width * h:width * h + width, :], ones[:, 0:width],
                                                  esum[p][:, h, 512 * half:512 * half + 512], start=True, stop=True,
                                                  skip_group_check=True,
                                                  tile_position=(0, width * h) if width < P else None)
                    mm.then_inc(full, 1)
                if kind == "proj" and final != "gamma":
                    half = step[2]
                    pe.wait_ge(norm_done, b.times(n_norm, n_norm))
                    for g in range(n_g):
                        mm = nc.tensor.matmul(dst[:, :], W["proj"][g], half_of(osb[g], half), start=(g == 0), stop=(g == n_g - 1))
                    mm.then_inc(full, 1)

            pe.wait_ge(const_ready, n_const)
            walk(pe, plan, do)

        @block.scalar
        def _(act):
            def do(step, image, bank):
                kind, b = step[0], image.plus(step[1])
                p = b.parity
                if kind == "qk":
                    t = step[2]
                    act.wait_ge(bank_full[bank[0]], bank[1])
                    if since(b, -1):
                        act.wait_ge(q_split, b.times(2, t // 2 - 1))
                    nc.scalar.activation(qkf[:, t // 2, 512 * (t % 2):512 * (t % 2) + 512], bk[bank[0]][:, :], ACT.Identity,
                                         bias=bias["qk"][t // 2], scale=scale_q if t < 2 else 1.0).then_inc(bank_free[bank[0]], 1)
                    act.wait_ge(bank_free[bank[0]], bank[1])
                    act.sem_inc(qk_evacuated, 1)
                if kind == "dqk":
                    w, h, half = step[2:]
                    act.wait_ge(bank_full[bank[0]], bank[1])
                    nc.scalar.activation(dq[w][p][0:64, h, 512 * half:512 * half + 512], bk[bank[0]][0:64, :], ACT.Identity,
                                         bias=bias["dqk"][w], scale=bias["dscale"] if w == 0 else 1.0).then_inc(bank_free[bank[0]], 1)
                    act.wait_ge(bank_free[bank[0]], bank[1])
                    act.sem_inc(dqk_ready, 1)
                if kind == "scores":
                    g, kc, h = step[2:]
                    u = plan.unit(g, kc, h)
                    q = plan.quad(g, kc)
                    act.wait_ge(scores_ready, b.times(plan.units, u + 1))
                    if h == 0 and not (isinstance(b.k, int) and 2 * b.k + b.p == 0 and q < 2):
                        act.wait_ge(pv_done, b.times(plan.quads, q - 1))
                        if D and (G[g].kind == "D" or g == 0):
                            two_ago = b.times(KC * D, (kc - 1) * D)
                            if (G[g].kind == "D" or kc < 2) and some(two_ago):
                                act.wait_ge(esum_done, two_ago)
                    nc.scalar.activation(e[q % 2][:, h, :], st[u % 2][:, :], ACT.Exp).then_inc(exp_done, 1)
                if kind == "evacuate":
                    g = step[2]
                    act.wait_ge(pv_done, b.times(plan.quads, plan.quad(g, KC - 1) + 1))
                    if since(b, -1):
                        act.wait_ge(y_ready, b.times(2))
                    nc.scalar.activation(osb[g][:, :], po[:, :, :].rearrange("p a b -> p (a b)"), ACT.Copy).then_inc(evacuated, 1)
                if kind == "norm":
                    g, half = step[2:]
                    number = 2 * g + half
                    act.wait_ge(bank_full[bank[0]], bank[1])
                    if some(b.times(n_norm, number - 1)):
                        act.wait_ge(norm_done, b.times(n_norm, number - 1))
                    nc.scalar.activation(r[:, half, :], bk[bank[0]][:, :], ACT.Ln).then_inc(bank_free[bank[0]], 1)
                    act.wait_ge(bank_free[bank[0]], bank[1])
                    act.sem_inc(ln_done, 1)
                    nc.scalar.activation(r[:, half, :], r[:, half, :], ACT.Exp, scale=-1.0).then_inc(recip_ready, 1)

            walk(act, plan, do)

        @block.vector
        def _(dve):
            def do(step, image, bank):
                kind, b = step[0], image.plus(step[1])
                p = b.parity
                if bank is not None and kind in ("v", "vd", "max", "turn", "proj"):
                    src, free = bk[bank[0]], bank_free[bank[0]]
                    dve.wait_ge(bank_full[bank[0]], bank[1])
                if kind in ("v", "vd"):
                    t = step[2]
                    if t == 0 and since(b, -2):
                        dve.wait_ge(pv_done, b.plus(-1).times(plan.quads))
                    if kind == "v":
                        nc.vector.tensor_copy(vs[p][:, 4 * t:4 * t + 4, :, 0:16],
                                              src[:, :].rearrange("p (c h d) -> p c h d", c=4, d=16)).then_inc(free, 1)
                    else:
                        nc.vector.tensor_copy(vd[p][:, 4 * t:4 * t + 4, :],
                                              src[:, :].rearrange("p (c m) -> p c m", c=4)).then_inc(free, 1)
                    dve.wait_ge(free, bank[1])
                    dve.sem_inc(v_ready, 1)
                if kind == "max":
                    g, h, qc, half = step[2:]
                    if (h, qc, half) == (0, 0, 0) and (g or since(b, -1)):
                        dve.wait_ge(negmax_ready, b.times(n_g, g))
                    nc.vector.tensor_reduce(mx[:, h * KC + qc, half:half + 1], src[:, :], AX.X, ALU.max).then_inc(free, 1)
                    if (h, qc, half) == (G[g].heads - 1, KC - 1, 1):
                        dve.wait_ge(free, bank[1])
                        dve.wait_ge(bank_free[1 - bank[0]], bank[1] if bank[0] else bank[1] - 1)
                        if g or since(b, -1):
                            dve.wait_ge(turned_ready, b.times(n_g, g))
                        rows = G[g].heads * KC
                        nc.vector.tensor_reduce(negm[:, 0:rows], mx[:, 0:rows, :], AX.X, ALU.max, negate=True).then_inc(negmax_ready, 1)
                if kind == "turn":
                    g = step[2]
                    if G[g].kind == "S":
                        n_s = len(plan.s_groups)
                        if g or since(b, -1):
                            dve.wait_ge(smax_ready, b.times(32 * n_s, 32 * g))
                        nc.vector.tensor_copy(top[:, :], src[:, 0:P]).then_inc(top_ready, 1)
                        dve.wait_ge(top_ready, b.times(n_s, g + 1))
                        nc.vector.tensor_tensor(low[:, :], src[:, 0:P], top[:, :], ALU.subtract).then_inc(free, 1)
                    else:
                        if since(b, -1):
                            dve.wait_ge(dmax_ready, b.times(16))
                        nc.vector.tensor_copy(turned[:, :], src[:, 0:P]).then_inc(free, 1)
                    dve.wait_ge(free, bank[1])
                    dve.sem_inc(turned_ready, 1)
                if kind == "scale":
                    g, half = step[2:]
                    number = 2 * g + half
                    dst = osb[g]
                    dve.wait_ge(recip_ready, b.times(n_norm, number + 1))
                    nc.vector.tensor_tensor(dst[:, 512 * half:512 * half + 512], osb[g][:, 512 * half:512 * half + 512],
                                            r[:, half, :], ALU.mult).then_inc(norm_done, 1)
                if kind == "proj":
                    half = step[2]
                    cut = slice(512 * half, 512 * half + 512)
                    if half == 0:
                        if since(b, -1):
                            dve.wait_ge(stored, b.times(16))
                        if res is not None:
                            dve.wait_ge(res_loaded, b.times(16, 16))
                    if final == "bias":
                        nc.vector.scalar_tensor_tensor(out=y[:, cut], in0=src[:, :], scalar=bias["out"], in1=res[:, cut],
                                                       op0=ALU.add, op1=ALU.add).then_inc(free, 1)
                    elif final == "plain":
                        nc.vector.tensor_copy(y[:, cut], src[:, :]).then_inc(free, 1)
                    else:
                        dve.wait_ge(norm_done, b.times(n_norm, half + 1))
                        nc.vector.tensor_scalar(osb[0][:, cut], osb[0][:, cut], bias["v"], bias["gamma"], ALU.add, ALU.mult).then_inc(y_step, 1)
                        dve.wait_ge(y_step, b.times(2, half + 1))
                        nc.vector.tensor_tensor(y[:, cut], osb[0][:, cut], res[:, cut], ALU.add).then_inc(y_ready, 1)
                    if final != "gamma":
                        dve.wait_ge(free, bank[1])
                        dve.sem_inc(y_ready, 1)

            if S:
                for p in range(2):
                    nc.vector.memset(stack[1][p][96:98, :, :], 1.0).then_inc(const_ready, 1)
                    nc.vector.memset(vs[p][:, :, :, 16:32], 0.0).then_inc(const_ready, 1)
                dve.wait_ge(const_ready, 4)
                for p in range(2):
                    nc.vector.memset(vs[p][:, :, :, 16:17], 1.0).then_inc(const_ready, 1)
            if D:
                for p in range(1 if S else 2):
                    nc.vector.memset(dq[1][p][64:65, :, :], 1.0).then_inc(const_ready, 1)
            nc.vector.memset(negm[:, :], 0.0).then_inc(const_ready, 1)

            walk(dve, plan, do)


def pipeline(eng, stages, do, images=NB):
    lag = max(x for _, x in stages)

    def turn(k, p):
        for name, late in stages:
            b = Batch(k, p - late)
            if isinstance(k, int) and not 0 <= 2 * k + b.p < images:
                continue
            do(name, b)

    whole = min((lag + 3) // 2 * 2, images)
    for t in range(whole):
        turn(t // 2, t % 2)
    if whole < images:
        with eng.Fori(whole // 2, images // 2) as k:
            turn(k, 0)
            turn(k, 1)
    for t in range(images, images + lag):
        turn(t // 2, t % 2)


def before(b, n=1):
    return not (isinstance(b.k, int) and 2 * b.k + b.p - n < 0)


def statistics(nc, tag, shared, x_in, images, mean, cov):
    with ExitStack() as ctx:
        sb = lambda name, shape: ctx.enter_context(nc.sbuf_tensor(f"{tag}_{name}", shape, F32))
        sem = lambda name: nc.alloc_semaphore(f"{tag}_{name}")
        pairs = shared["bank_pairs"]
        x = [sb(f"x{p}", [P, N]) for p in range(2)]
        xc = [sb(f"xc{p}", [P, N]) for p in range(2)]
        xt = [sb(f"xt{p}", [P, 2, 512]) for p in range(2)]
        total = sb("total", [P, images])
        minus = [sb(f"minus{p}", [P, 1]) for p in range(2)]
        apart = sb("apart", [P, P])
        apart_t = sb("apart_t", [P, P])
        turned = [[pairs[p][:, h, :] for h in range(2)] for p in range(2)]
        gram = [pairs[2][:, p, :] for p in range(2)]
        loaded, summed, minus_ready, centred = [sem(f"loaded{p}") for p in range(2)], sem("summed"), sem("minus_ready"), sem("centred")
        turned_ready, copied, gram_ready, added = sem("turned_ready"), sem("copied"), sem("gram_ready"), sem("added")
        end_step, end_turned, end_copied, end_gram = sem("end_step"), sem("end_turned"), sem("end_copied"), sem("end_gram")
        block = ctx.enter_context(nc.Block())
        ident = shared["ident"]
        stages = [("load", 0), ("centre", 0), ("turn", 1), ("gram", 2)]

        @block.sync
        def _(sp):
            def do(name, b):
                if name == "load":
                    row = sp.snap(b.plus(0).k * 2 + b.p) if not isinstance(b.k, int) else 2 * b.k + b.p
                    if before(b, 2):
                        sp.wait_ge(centred, b.times(1, -1))
                    sp.dma_start(x[b.parity][:, :], x_in[row]).then_inc(loaded[b.parity], 16)
            pipeline(sp, stages, do, images)

        @block.vector
        def _(dve):
            def do(name, b):
                if name == "centre":
                    dve.wait_ge(loaded[b.parity], b.pairs(16))
                    if before(b, 2):
                        dve.wait_ge(centred, b.times(1, -1))
                    nc.vector.tensor_reduce(minus[b.parity][:, :], x[b.parity][:, :], AX.X, ALU.add).then_inc(summed, 1)
                    dve.wait_ge(summed, b.times(1, 1))
                    nc.vector.tensor_scalar(minus[b.parity][:, :], minus[b.parity][:, :], -1.0 / N, None, ALU.mult).then_inc(minus_ready, 1)
                if name == "gram":
                    dve.wait_ge(gram_ready, b.times(1, 1))
                    if before(b, 1):
                        dve.wait_ge(added, b.times(1))
                        nc.vector.tensor_tensor(cov, gram[b.parity][:, 0:P], cov, ALU.add).then_inc(added, 1)
                    else:
                        nc.vector.tensor_copy(cov, gram[b.parity][:, 0:P]).then_inc(added, 1)
            pipeline(dve, stages, do, images)
            dve.wait_ge(end_copied, images)
            nc.vector.memset(apart[:, :], 0.0).then_inc(end_step, 1)
            nc.vector.tensor_reduce(mean, total[:, :], AX.X, ALU.add).then_inc(end_step, 1)
            dve.wait_ge(end_step, 2)
            nc.vector.tensor_scalar(mean, mean, -1.0 / images, None, ALU.mult).then_inc(end_step, 1)
            dve.wait_ge(end_step, 3)
            nc.vector.tensor_scalar(apart[:, 0:images], total[:, :], mean, None, ALU.add).then_inc(end_step, 1)
            dve.wait_ge(end_turned, 1)
            nc.vector.tensor_copy(apart_t[:, :], turned[0][0][:, 0:P]).then_inc(end_step, 1)
            dve.wait_ge(end_gram, 1)
            dve.wait_ge(added, images)
            nc.vector.tensor_scalar(cov, cov, 1.0 / N, None, ALU.mult).then_inc(end_step, 1)
            dve.wait_ge(end_step, 6)
            nc.vector.tensor_tensor(cov, gram[0][:, 0:P], cov, ALU.add).then_inc(end_step, 1)
            dve.wait_ge(end_step, 7)
            nc.vector.tensor_scalar(cov, cov, 1.0 / images, None, ALU.mult).then_inc(end_step, 1)

        @block.gpsimd
        def _(pool):
            def do(name, b):
                if name == "centre":
                    pool.wait_ge(minus_ready, b.times(1, 1))
                    if isinstance(b.k, int):
                        at = 2 * b.k + b.p
                        dst = total[:, at:at + 1]
                    else:
                        dst = total[:, bass.ds(b.k * 2 + b.p, 1)]
                    nc.gpsimd.tensor_tensor(dst, minus[b.parity][:, :], shared["zero"], ALU.subtract).then_inc(end_copied, 1)
            pipeline(pool, stages, do, images)

        @block.scalar
        def _(act):
            def do(name, b):
                if name == "centre":
                    act.wait_ge(minus_ready, b.times(1, 1))
                    if before(b, 2):
                        act.wait_ge(turned_ready, b.times(2, -2))
                    act.wait_ge(end_copied, b.times(1, 1))
                    nc.scalar.activation(xc[b.parity][:, :], x[b.parity][:, :], ACT.Identity, bias=minus[b.parity][:, :]).then_inc(centred, 1)
                if name == "turn":
                    for half in range(2):
                        act.wait_ge(turned_ready, b.times(2, half + 1))
                        if before(b, 2):
                            act.wait_ge(gram_ready, b.times(1, -1))
                        nc.scalar.activation(xt[b.parity][:, half, :], turned[b.parity][half][:, :], ACT.Copy).then_inc(copied, 1)
            pipeline(act, stages, do, images)

        @block.tensor
        def _(pe):
            def do(name, b):
                if name == "turn":
                    pe.wait_ge(centred, b.times(1, 1))
                    for half in range(2):
                        if before(b, 2):
                            pe.wait_ge(copied, b.times(2, half - 3))
                        for c in range(4):
                            at = 512 * half + P * c
                            mm = nc.tensor.transpose(turned[b.parity][half][:, P * c:P * c + P], xc[b.parity][:, at:at + P], ident)
                        mm.then_inc(turned_ready, 1)
                if name == "gram":
                    pe.wait_ge(copied, b.times(2, 2))
                    if before(b, 2):
                        pe.wait_ge(added, b.times(1, -1))
                    for c in range(KC):
                        block_t = xt[b.parity][:, c // 4, P * (c % 4):P * (c % 4) + P]
                        mm = nc.tensor.matmul(gram[b.parity][:, 0:P], block_t, block_t, start=(c == 0), stop=(c == KC - 1))
                    mm.then_inc(gram_ready, 1)
            pipeline(pe, stages, do, images)
            pe.wait_ge(end_step, 4)
            pe.wait_ge(copied, 2 * images)
            nc.tensor.transpose(turned[0][0][:, 0:P], apart[:, :], ident).then_inc(end_turned, 1)
            pe.wait_ge(end_step, 5)
            pe.wait_ge(added, images)
            nc.tensor.matmul(gram[0][:, 0:P], apart_t[:, :], apart_t[:, :], start=True, stop=True).then_inc(end_gram, 1)


def whiten(nc, M, shared, mean, cov, move, offset):
    with ExitStack() as ctx:
        sb = lambda name, shape: ctx.enter_context(nc.sbuf_tensor(f"w_{name}", shape, F32))
        sem = lambda name: nc.alloc_semaphore(f"w_{name}")
        a = sb("a", [P, 2, P])
        own = sb("own", [P, P])
        diagonal = sb("diagonal", [P, 2])
        trace = sb("trace", [P, 2])
        inverse = sb("inverse", [P, 2])
        ratio = sb("ratio", [P, 1])
        root = sb("root", [P, 1])
        power = sb("power", [P, 1])
        three = sb("three", [P, P])
        ridge = sb("ridge", [P, P])
        yz = sb("yz", [P, 2, 2, P])
        t = sb("t", [P, 2, P])
        p_trace, p_t, p_yz, p_end = [shared["bank_pairs"][i // 2][:, i % 2, :] for i in range(4)]
        setup, diagonal_ready, trace_ready, first_ready = sem("setup"), sem("diagonal_ready"), sem("trace_ready"), sem("first_ready")
        zy_made, t_ready, yz_made, yz_ready = sem("zy_made"), sem("t_ready"), sem("yz_made"), sem("yz_ready")
        ratio_ready, root_ready, product, moved, offset_made = (
            sem("ratio_ready"), sem("root_ready"), sem("product"), sem("moved"), sem("offset_made"))
        block = ctx.enter_context(nc.Block())

        @block.vector
        def _(dve):
            nc.vector.memset(power[:, :], 0.5).then_inc(ratio_ready, 1)
            nc.vector.tensor_scalar(three[:, :], M["ident"], 0.75, None, ALU.mult).then_inc(setup, 1)
            nc.vector.tensor_scalar(ridge[:, :], M["ident"], EPS_COV, None, ALU.mult).then_inc(setup, 1)
            for s in range(2):
                nc.vector.tensor_tensor(a[:, s, :], cov[s], M["block"], ALU.mult).then_inc(setup, 1)
            dve.wait_ge(setup, 4)
            for s in range(2):
                nc.vector.tensor_tensor(a[:, s, :], a[:, s, :], ridge[:, :], ALU.add).then_inc(setup, 1)
            dve.wait_ge(setup, 6)
            for s in range(2):
                nc.vector.tensor_tensor(own[:, :], a[:, s, :], M["ident"], ALU.mult).then_inc(setup, 1)
                dve.wait_ge(setup, 7 + 2 * s)
                nc.vector.tensor_reduce(diagonal[:, s:s + 1], own[:, :], AX.X, ALU.add).then_inc(setup, 1)
                dve.wait_ge(setup, 8 + 2 * s)
            nc.vector.tensor_copy(yz[:, 0, 1, :], M["ident"]).then_inc(diagonal_ready, 1)
            nc.vector.tensor_copy(yz[:, 1, 1, :], M["ident"]).then_inc(diagonal_ready, 1)
            dve.wait_ge(trace_ready, 1)
            nc.vector.tensor_copy(trace[:, :], p_trace[:, 0:2]).then_inc(setup, 1)
            dve.wait_ge(setup, 11)
            nc.vector.reciprocal(inverse[:, :], trace[:, :]).then_inc(setup, 1)
            dve.wait_ge(setup, 12)
            for s in range(2):
                nc.vector.tensor_scalar(yz[:, s, 0, :], a[:, s, :], inverse[:, s:s + 1], None, ALU.mult).then_inc(yz_ready if s else first_ready, 1)
            nc.vector.tensor_tensor(ratio[:, :], trace[:, 1:2], inverse[:, 0:1], ALU.mult).then_inc(ratio_ready, 1)
            with dve.Fori(0, ROOT_STEPS) as k:
                dve.wait_ge(zy_made, k + 1)
                for s in range(2):
                    nc.vector.scalar_tensor_tensor(out=t[:, s, :], in0=p_t[:, P * s:P * s + P], scalar=-0.25, in1=three[:, :],
                                                   op0=ALU.mult, op1=ALU.add).then_inc(t_ready, 1)
                dve.wait_ge(yz_made, k + 1)
                nc.vector.tensor_copy(yz[:, :, :, :].rearrange("p s y c -> p (s y c)"), p_yz[:, :]).then_inc(yz_ready, 1)
            dve.wait_ge(product, 1)
            dve.wait_ge(root_ready, 1)
            nc.vector.tensor_scalar(move, p_end[:, 0:P], root[:, :], None, ALU.mult).then_inc(moved, 1)
            dve.wait_ge(offset_made, 1)
            nc.vector.tensor_tensor(offset, mean[1], p_trace[:, 0:1], ALU.subtract).then_inc(moved, 1)

        @block.gpsimd
        def _(pool):
            pool.wait_ge(ratio_ready, 2)
            nc.gpsimd.tensor_tensor(root[:, :], ratio[:, :], power[:, :], ALU.pow).then_inc(root_ready, 1)

        @block.tensor
        def _(pe):
            pe.wait_ge(diagonal_ready, 2)
            nc.tensor.matmul(p_trace[:, 0:2], M["block"], diagonal[:, :], start=True, stop=True).then_inc(trace_ready, 1)
            pe.wait_ge(first_ready, 1)
            with pe.Fori(0, ROOT_STEPS) as k:
                pe.wait_ge(yz_ready, k + 1)
                for s in range(2):
                    mm = nc.tensor.matmul(p_t[:, P * s:P * s + P], yz[:, s, 1, :], yz[:, s, 0, :], start=True, stop=True)
                mm.then_inc(zy_made, 1)
                pe.wait_ge(t_ready, k * 2 + 2)
                for s in range(2):
                    for part in range(2):
                        dst, m = p_yz[:, P * (2 * s + part):P * (2 * s + part) + P], yz[:, s, part, :]
                        nc.tensor.matmul(dst, m, t[:, s, :], start=True, stop=False)
                        mm = nc.tensor.matmul(dst, t[:, s, :], m, start=False, stop=True)
                mm.then_inc(yz_made, 1)
            pe.wait_ge(yz_ready, ROOT_STEPS + 1)
            nc.tensor.matmul(p_end[:, 0:P], yz[:, 0, 1, :], yz[:, 1, 0, :], start=True, stop=True).then_inc(product, 1)
            pe.wait_ge(moved, 1)
            nc.tensor.matmul(p_trace[:, 0:1], move, mean[0], start=True, stop=True).then_inc(offset_made, 1)


class GroupNorm:

    def __init__(self, sb, name, gain, shift):
        self.parts = [sb(f"{name}_parts{p}", [P, 12]) for p in range(2)]
        self.pair = [sb(f"{name}_pair{p}", [P, 2]) for p in range(2)]
        self.group = [sb(f"{name}_group{p}", [P, 2]) for p in range(2)]
        self.var = [sb(f"{name}_var{p}", [P, 1]) for p in range(2)]
        self.rstd = [sb(f"{name}_rstd{p}", [P, 1]) for p in range(2)]
        self.a = [sb(f"{name}_a{p}", [P, 1]) for p in range(2)]
        self.b = [sb(f"{name}_b{p}", [P, 1]) for p in range(2)]
        self.gain, self.shift = gain, shift


GN_STEPS = 10


def norm_statistics(nc, dve, g, p, x, b, step, begun):
    at = lambda n: b.times(GN_STEPS, n)
    nc.vector.bn_stats(g.parts[p][:, 0:6], x[:, 0:512]).then_inc(step, 1)
    nc.vector.bn_stats(g.parts[p][:, 6:12], x[:, 512:N]).then_inc(step, 1)
    dve.wait_ge(step, at(2))
    dve.sem_inc(begun, 1)
    nc.vector.bn_aggr(g.pair[p][:, :], g.parts[p][:, :]).then_inc(step, 1)
    dve.wait_ge(step, at(3))
    nc.vector.scalar_tensor_tensor(out=g.pair[p][:, 1:2], in0=g.pair[p][:, 0:1], scalar=g.pair[p][:, 0:1],
                                   in1=g.pair[p][:, 1:2], op0=ALU.mult, op1=ALU.add).then_inc(step, 1)


def norm_variance(nc, dve, g, p, ps, b, step):
    at = lambda n: b.times(GN_STEPS, n)
    nc.vector.tensor_copy(g.group[p][:, :], ps).then_inc(step, 1)
    dve.wait_ge(step, at(5))
    nc.vector.scalar_tensor_tensor(out=g.var[p][:, :], in0=g.group[p][:, 0:1], scalar=g.group[p][:, 0:1],
                                   in1=g.group[p][:, 1:2], op0=ALU.mult, op1=ALU.subtract).then_inc(step, 1)
    dve.wait_ge(step, at(6))
    nc.vector.tensor_scalar(g.var[p][:, :], g.var[p][:, :], -1.0, EPS_GN, ALU.mult, ALU.add).then_inc(step, 1)


def norm_factors(nc, dve, g, p, b, step):
    at = lambda n: b.times(GN_STEPS, n)
    nc.vector.tensor_tensor(g.a[p][:, :], g.rstd[p][:, :], g.gain, ALU.mult).then_inc(step, 1)
    dve.wait_ge(step, at(8))
    nc.vector.scalar_tensor_tensor(out=g.b[p][:, :], in0=g.group[p][:, 0:1], scalar=g.a[p][:, :], in1=g.shift,
                                   op0=ALU.mult, op1=ALU.subtract).then_inc(step, 1)
    dve.wait_ge(step, at(9))
    nc.vector.tensor_scalar(g.b[p][:, :], g.b[p][:, :], -1.0, None, ALU.mult).then_inc(step, 1)


def gate(nc, M, V, shared, halves, move, offset, x_in, pos_in, h_out, normed_out, gated_out):
    with ExitStack() as ctx:
        sb = lambda name, shape: ctx.enter_context(nc.sbuf_tensor(f"g_{name}", shape, F32))
        sem = lambda name: nc.alloc_semaphore(f"g_{name}")
        pair = lambda name, shape: [sb(f"{name}{p}", shape) for p in range(2)]
        flat = lambda t: t[:, :, :].rearrange("p a b -> p (a b)")
        x0, h, xg, xs = pair("x0", [P, N]), pair("h", [P, N]), pair("xg", [P, N]), pair("xs", [P, N])
        pos = sb("pos", [P, N])
        th1, u1 = sb("th1", [96, N]), sb("u1", [96, N])
        field = sb("field", [96, SIDE + 2, SIDE])
        th2, u2, s2 = sb("th2", [64, 512]), sb("u2", [64, 512]), sb("s2", [64, 512])
        th3, gated, normed = sb("th3", [P, N]), sb("gated", [P, N]), sb("normed", [P, N])
        power = sb("power", [P, 1])
        g1, g2 = GroupNorm(sb, "g1", V["c_pre_g"], V["c_pre_b"]), GroupNorm(sb, "g2", V["c_norm_g"], V["c_norm_b"])
        p_h, p_s1, p_s3, small = shared["bank_pairs"]
        p_s2, p_g = small[:, 0:1, :], small[:, 1:2, :]
        const_ready, pos_loaded, loaded, h_made, h_ready, h_stored = (
            sem("const_ready"), sem("pos_loaded"), [sem(f"loaded{p}") for p in range(2)], sem("h_made"), sem("h_ready"),
            [sem(f"h_stored{p}") for p in range(2)])
        step1, step2, group1, group2, rstd1, rstd2 = (
            sem("step1"), sem("step2"), sem("group1"), sem("group2"), sem("rstd1"), sem("rstd2"))
        xg_ready, x_ready = sem("xg_ready"), sem("x_ready")
        s1_made, th1_ready, u1_ready, field_ready = sem("s1_made"), sem("th1_ready"), sem("u1_ready"), sem("field_ready")
        s2_made, th2_ready, u2_ready, s2_ready = sem("s2_made"), sem("th2_ready"), sem("u2_ready"), sem("s2_ready")
        s3_made, th3_ready, gated_ready, normed_ready = sem("s3_made"), sem("th3_ready"), sem("gated_ready"), sem("normed_ready")
        gated_stored, normed_stored = sem("gated_stored"), sem("normed_stored")
        block = ctx.enter_context(nc.Block())
        stages = [("load", 0), ("move", 1), ("conv1", 2), ("stats1", 1), ("stats2", 2), ("field", 2), ("factors1", 1),
                  ("conv2", 2), ("factors2", 2), ("norm1", 1), ("conv3", 2), ("out", 2)]

        @block.sync
        def _(sp):
            sp.dma_start(pos[:, :], pos_in).then_inc(pos_loaded, 16)

            def do(name, b):
                p = b.parity
                if name not in ("load", "stats1", "out"):
                    return
                row = 2 * b.k + b.p if isinstance(b.k, int) else sp.snap(b.k * 2 + b.p)
                if name == "load":
                    if before(b, 2):
                        sp.wait_ge(h_made, b.times(1, -1))
                    sp.dma_start(x0[p][:, :], x_in[row]).then_inc(loaded[p], 16)
                if name == "stats1":
                    sp.wait_ge(h_ready, b.times(1, 1))
                    sp.dma_start(h_out[row], h[p][:, :]).then_inc(h_stored[p], 16)
                if name == "out":
                    sp.wait_ge(gated_ready, b.times(1, 1))
                    sp.dma_start(gated_out[row], gated[:, :]).then_inc(gated_stored, 16)
                    sp.wait_ge(normed_ready, b.times(1, 1))
                    sp.dma_start(normed_out[row], normed[:, :]).then_inc(normed_stored, 16)
            pipeline(sp, stages, do)
            for stored, n in ((h_stored[0], NB // 2), (h_stored[1], NB // 2), (gated_stored, NB), (normed_stored, NB)):
                sp.wait_ge(stored, 16 * n)

        @block.gpsimd
        def _(pool):
            def do(name, b):
                p = b.parity
                if name in ("factors1", "factors2"):
                    g, step, rstd = (g1, step1, rstd1) if name == "factors1" else (g2, step2, rstd2)
                    pool.wait_ge(step, b.times(GN_STEPS, 7))
                    nc.gpsimd.tensor_tensor(g.rstd[p][:, :], g.var[p][:, :], power[:, :], ALU.pow).then_inc(rstd, 1)
                if name == "norm1":
                    pool.wait_ge(xg_ready, b.times(1, 1))
                    if before(b, 2):
                        pool.wait_ge(gated_ready, b.times(1, -1))
                        pool.wait_ge(normed_ready, b.times(1, -1))
                    nc.gpsimd.tensor_tensor(xs[p][:, :], xg[p][:, :], pos[:, :], ALU.add).then_inc(x_ready, 1)
            pool.wait_ge(pos_loaded, 16)
            pool.wait_ge(const_ready, 2)
            pipeline(pool, stages, do)

        @block.tensor
        def _(pe):
            half_of = lambda t, half: t[:, 512 * half:512 * half + 512]

            def do(name, b):
                p = b.parity
                if name == "move":
                    pe.wait_ge(loaded[p], b.pairs(16))
                    if before(b, 1):
                        pe.wait_ge(h_ready, b.times(1))
                    for half in range(2):
                        mm = nc.tensor.matmul(p_h[:, half, :], move, half_of(x0[p], half), start=True, stop=True)
                    mm.then_inc(h_made, 1)
                if name == "stats1":
                    pe.wait_ge(step1, b.times(GN_STEPS, 4))
                    nc.tensor.matmul(p_g[:, 0, 0:2], M["mean4"], g1.pair[p][:, :], start=True, stop=True).then_inc(group1, 1)
                if name == "stats2":
                    pe.wait_ge(step2, b.times(GN_STEPS, 4))
                    if before(b, 1):
                        pe.wait_ge(th3_ready, b.times(1))
                    nc.tensor.matmul(p_s3[:, 0, 0:2], M["mean4"], g2.pair[p][:, :], start=True, stop=True).then_inc(group2, 1)
                if name == "conv1":
                    pe.wait_ge(x_ready, b.times(1, 1))
                    if before(b, 1):
                        pe.wait_ge(th1_ready, b.times(1))
                        pe.wait_ge(u1_ready, b.times(1))
                    for half in range(2):
                        mm = nc.tensor.matmul(p_s1[0:96, half, :], M["c_s1"], half_of(xs[p], half), start=True, stop=True)
                    mm.then_inc(s1_made, 1)
                if name == "conv2":
                    pe.wait_ge(field_ready, b.times(3, 3))
                    if before(b, 1):
                        pe.wait_ge(th2_ready, b.times(1))
                        pe.wait_ge(u2_ready, b.times(1))
                    for half in range(2):
                        for dy in range(3):
                            at = SIDE // 2 * half + dy
                            rows = field[:, at:at + SIDE // 2, :].rearrange("p a b -> p (a b)")
                            mm = nc.tensor.matmul(p_s2[32 * half:32 * half + 32, 0, :], M[f"c_s2{dy}"], rows,
                                                  start=(dy == 0), stop=(dy == 2), tile_position=(0, 32 * half),
                                                  skip_group_check=True)
                    mm.then_inc(s2_made, 1)
                if name == "conv3":
                    pe.wait_ge(s2_ready, b.times(1, 1))
                    pe.wait_ge(step2, b.times(GN_STEPS, 5))
                    for half in range(2):
                        rows = slice(32 * half, 32 * half + 32)
                        mm = nc.tensor.matmul(p_s3[:, half, :], M["c_s3"][rows, :], s2[rows, :], start=True, stop=True)
                    mm.then_inc(s3_made, 1)
            pipeline(pe, stages, do)

        @block.scalar
        def _(act):
            def do(name, b):
                p = b.parity
                if name == "move":
                    act.wait_ge(h_made, b.times(1, 1))
                    if before(b, 2):
                        act.wait_ge(h_stored[p], b.plus(-2).pairs(16))
                    nc.scalar.activation(h[p][:, :], flat(p_h), ACT.Identity, bias=offset).then_inc(h_ready, 1)
                if name == "conv1":
                    act.wait_ge(s1_made, b.times(1, 1))
                    if before(b, 1):
                        act.wait_ge(field_ready, b.times(3))
                    nc.scalar.activation(th1[:, :], flat(p_s1)[0:96, :], ACT.Tanh, bias=halves[0], scale=0.5).then_inc(th1_ready, 1)
                if name == "conv2":
                    act.wait_ge(s2_made, b.times(1, 1))
                    if before(b, 1):
                        act.wait_ge(s2_ready, b.times(1))
                    nc.scalar.activation(th2[:, :], p_s2[0:64, 0, :], ACT.Tanh, bias=halves[1], scale=0.5).then_inc(th2_ready, 1)
                if name == "norm1":
                    act.wait_ge(step1, b.times(GN_STEPS, GN_STEPS))
                    if before(b, 2):
                        act.wait_ge(x_ready, b.times(1, -1))
                    nc.scalar.activation(xg[p][:, :], h[p][:, :], ACT.Identity, bias=g1.b[p][:, :], scale=g1.a[p][:, :]).then_inc(xg_ready, 1)
                if name == "conv3":
                    act.wait_ge(s3_made, b.times(1, 1))
                    if before(b, 1):
                        act.wait_ge(gated_ready, b.times(1))
                    nc.scalar.activation(th3[:, :], flat(p_s3), ACT.Tanh, bias=halves[2], scale=0.5).then_inc(th3_ready, 1)
                if name == "out":
                    act.wait_ge(step2, b.times(GN_STEPS, GN_STEPS))
                    if before(b, 1):
                        act.wait_ge(normed_stored, b.times(16))
                    nc.scalar.activation(normed[:, :], xs[p][:, :], ACT.Identity, bias=g2.b[p][:, :], scale=g2.a[p][:, :]).then_inc(normed_ready, 1)
            pipeline(act, stages, do)

        @block.vector
        def _(dve):
            nc.vector.memset(power[:, :], -0.5).then_inc(const_ready, 1)
            nc.vector.memset(field[:, :, :], 0.0).then_inc(const_ready, 1)
            dve.wait_ge(const_ready, 2)

            def do(name, b):
                p = b.parity
                if name == "stats1":
                    dve.wait_ge(h_ready, b.times(1, 1))
                    norm_statistics(nc, dve, g1, p, h[p], b, step1, const_ready)
                if name == "stats2":
                    norm_statistics(nc, dve, g2, p, xs[p], b, step2, const_ready)
                if name in ("factors1", "factors2"):
                    g, step, group, rstd, sums = (g1, step1, group1, rstd1, p_g) if name == "factors1" else (g2, step2, group2, rstd2, p_s3)
                    dve.wait_ge(group, b.times(1, 1))
                    norm_variance(nc, dve, g, p, sums[:, 0, 0:2], b, step)
                    dve.wait_ge(rstd, b.times(1, 1))
                    norm_factors(nc, dve, g, p, b, step)
                if name == "conv1":
                    dve.wait_ge(th1_ready, b.times(1, 1))
                    nc.vector.tensor_scalar(u1[:, :], flat(p_s1)[0:96, :], V["c_s1b"], 0.5, ALU.add, ALU.mult).then_inc(u1_ready, 1)
                if name == "field":
                    dve.wait_ge(u1_ready, b.times(1, 1))
                    if before(b, 1):
                        dve.wait_ge(s2_made, b.times(1))
                    for dx in range(3):
                        rows = slice(32 * dx, 32 * dx + 32)
                        dst, src = slice(max(0, 1 - dx), min(SIDE, SIDE + 1 - dx)), slice(max(0, dx - 1), min(SIDE, SIDE - 1 + dx))
                        a = th1[rows, :].rearrange("p (y x) -> p y x", x=SIDE)[:, :, src]
                        c = u1[rows, :].rearrange("p (y x) -> p y x", x=SIDE)[:, :, src]
                        nc.vector.scalar_tensor_tensor(out=field[rows, 1:SIDE + 1, dst], in0=a, scalar=1.0, in1=c,
                                                       op0=ALU.add, op1=ALU.mult).then_inc(field_ready, 1)
                if name == "conv2":
                    dve.wait_ge(th2_ready, b.times(1, 1))
                    nc.vector.tensor_scalar(u2[:, :], p_s2[0:64, 0, :], halves[3], 0.5, ALU.add, ALU.mult).then_inc(u2_ready, 1)
                    dve.wait_ge(u2_ready, b.times(1, 1))
                    if before(b, 1):
                        dve.wait_ge(s3_made, b.times(1))
                    nc.vector.scalar_tensor_tensor(out=s2[:, :], in0=th2[:, :], scalar=1.0, in1=u2[:, :],
                                                   op0=ALU.add, op1=ALU.mult).then_inc(s2_ready, 1)
                if name == "conv3":
                    dve.wait_ge(th3_ready, b.times(1, 1))
                    if before(b, 1):
                        dve.wait_ge(gated_stored, b.times(16))
                    nc.vector.scalar_tensor_tensor(out=gated[:, :], in0=th3[:, :], scalar=1.0, in1=xs[p][:, :],
                                                   op0=ALU.add, op1=ALU.mult).then_inc(gated_ready, 1)
            pipeline(dve, stages, do)


def feed_forward(nc, M, V, shared, half_b1, ff_in, h_in, out):
    with ExitStack() as ctx:
        sb = lambda name, shape: ctx.enter_context(nc.sbuf_tensor(f"f_{name}", shape, F32))
        sem = lambda name: nc.alloc_semaphore(f"f_{name}")
        pair = lambda name, shape: [sb(f"{name}{p}", shape) for p in range(2)]
        flat = lambda t: t[:, :, :].rearrange("p a b -> p (a b)")
        ff, h, th, u, s = pair("ff", [P, N]), pair("h", [P, N]), pair("th", [P, N]), pair("u", [P, N]), pair("s", [P, N])
        f2, fin, hb, z = pair("f2", [P, N]), pair("fin", [P, N]), pair("hb", [P, N]), pair("z", [P, N])
        power = sb("power", [P, 1])
        g = GroupNorm(sb, "g", V["c_post_g"], V["c_post_b"])
        p_2, p_3, p_g, _ = shared["bank_pairs"]
        const_ready, ff_loaded, h_loaded = sem("const_ready"), [sem(f"ff_loaded{p}") for p in range(2)], [sem(f"h_loaded{p}") for p in range(2)]
        th_ready, u_ready, s_ready, f2_made, f2_ready, f3_made, fin_ready = (
            sem("th_ready"), sem("u_ready"), sem("s_ready"), sem("f2_made"), sem("f2_ready"), sem("f3_made"), sem("fin_ready"))
        step, group, rstd, hb_ready, z_ready, stored = (
            sem("step"), sem("group"), sem("rstd"), sem("hb_ready"), sem("z_ready"), [sem(f"stored{p}") for p in range(2)])
        block = ctx.enter_context(nc.Block())
        stages = [("load", 0), ("final", 3), ("silu", 1), ("w2", 1), ("stats", 2), ("factors", 2), ("w3", 1)]

        @block.sync
        def _(sp):
            def do(name, b):
                p = b.parity
                if name not in ("load", "silu", "final"):
                    return
                row = 2 * b.k + b.p if isinstance(b.k, int) else sp.snap(b.k * 2 + b.p)
                if name == "load":
                    if before(b, 2):
                        sp.wait_ge(u_ready, b.times(1, -1))
                        sp.wait_ge(th_ready, b.times(1, -1))
                    sp.dma_start(ff[p][:, :], ff_in[row]).then_inc(ff_loaded[p], 16)
                if name == "silu":
                    if before(b, 2):
                        sp.wait_ge(hb_ready, b.times(1, -1))
                    sp.dma_start(h[p][:, :], h_in[row]).then_inc(h_loaded[p], 16)
                if name == "final":
                    sp.wait_ge(z_ready, b.times(1, 1))
                    sp.dma_start(out[row], z[p][:, :]).then_inc(stored[p], 16)
            pipeline(sp, stages, do)
            for p in range(2):
                sp.wait_ge(stored[p], 16 * NB // 2)

        @block.gpsimd
        def _(pool):
            def do(name, b):
                p = b.parity
                if name == "factors":
                    pool.wait_ge(step, b.times(GN_STEPS, 7))
                    nc.gpsimd.tensor_tensor(g.rstd[p][:, :], g.var[p][:, :], power[:, :], ALU.pow).then_inc(rstd, 1)
            pool.wait_ge(const_ready, 1)
            pipeline(pool, stages, do)

        @block.tensor
        def _(pe):
            half_of = lambda t, half: t[:, 512 * half:512 * half + 512]

            def do(name, b):
                p = b.parity
                if name == "w2":
                    pe.wait_ge(s_ready, b.times(1, 1))
                    if before(b, 1):
                        pe.wait_ge(f2_ready, b.times(1))
                    for half in range(2):
                        mm = nc.tensor.matmul(p_2[:, half, :], M["c_w2"], half_of(s[p], half), start=True, stop=True)
                    mm.then_inc(f2_made, 1)
                if name == "w3":
                    pe.wait_ge(f2_ready, b.times(1, 1))
                    if before(b, 1):
                        pe.wait_ge(fin_ready, b.times(1))
                    for half in range(2):
                        mm = nc.tensor.matmul(p_3[:, half, :], M["c_out"], half_of(f2[p], half), start=True, stop=True)
                    mm.then_inc(f3_made, 1)
                if name == "stats":
                    pe.wait_ge(step, b.times(GN_STEPS, 4))
                    if before(b, 1):
                        pe.wait_ge(step, b.times(GN_STEPS, 5 - GN_STEPS))
                    nc.tensor.matmul(p_g[:, 0, 0:2], M["mean4"], g.pair[p][:, :], start=True, stop=True).then_inc(group, 1)
            pipeline(pe, stages, do)

        @block.scalar
        def _(act):
            def do(name, b):
                p = b.parity
                if name == "silu":
                    act.wait_ge(ff_loaded[p], b.pairs(16))
                    if before(b, 2):
                        act.wait_ge(s_ready, b.times(1, -1))
                    nc.scalar.activation(th[p][:, :], ff[p][:, :], ACT.Tanh, bias=half_b1, scale=0.5).then_inc(th_ready, 1)
                if name == "w2":
                    act.wait_ge(f2_made, b.times(1, 1))
                    if before(b, 2):
                        act.wait_ge(f3_made, b.times(1, -1))
                    nc.scalar.activation(f2[p][:, :], flat(p_2), ACT.Identity, bias=V["c_ff_b2"]).then_inc(f2_ready, 1)
                if name == "w3":
                    act.wait_ge(f3_made, b.times(1, 1))
                    if before(b, 2):
                        act.wait_ge(z_ready, b.times(1, -1))
                    nc.scalar.activation(fin[p][:, :], flat(p_3), ACT.Identity, bias=V["c_out_b"]).then_inc(fin_ready, 1)
                if name == "factors":
                    act.wait_ge(step, b.times(GN_STEPS, GN_STEPS))
                    act.wait_ge(h_loaded[p], b.pairs(16))
                    if before(b, 2):
                        act.wait_ge(z_ready, b.times(1, -1))
                    nc.scalar.activation(hb[p][:, :], h[p][:, :], ACT.Identity, bias=g.b[p][:, :]).then_inc(hb_ready, 1)
            pipeline(act, stages, do)

        @block.vector
        def _(dve):
            nc.vector.memset(power[:, :], -0.5).then_inc(const_ready, 1)

            def do(name, b):
                p = b.parity
                if name == "silu":
                    dve.wait_ge(ff_loaded[p], b.pairs(16))
                    if before(b, 2):
                        dve.wait_ge(s_ready, b.times(1, -1))
                    nc.vector.tensor_scalar(u[p][:, :], ff[p][:, :], V["c_ff_b1"], 0.5, ALU.add, ALU.mult).then_inc(u_ready, 1)
                    dve.wait_ge(u_ready, b.times(1, 1))
                    dve.wait_ge(th_ready, b.times(1, 1))
                    if before(b, 2):
                        dve.wait_ge(f2_made, b.times(1, -1))
                    nc.vector.scalar_tensor_tensor(out=s[p][:, :], in0=th[p][:, :], scalar=1.0, in1=u[p][:, :],
                                                   op0=ALU.add, op1=ALU.mult).then_inc(s_ready, 1)
                if name == "stats":
                    dve.wait_ge(fin_ready, b.times(1, 1))
                    norm_statistics(nc, dve, g, p, fin[p], b, step, const_ready)
                if name == "factors":
                    dve.wait_ge(group, b.times(1, 1))
                    norm_variance(nc, dve, g, p, p_g[:, 0, 0:2], b, step)
                    dve.wait_ge(rstd, b.times(1, 1))
                    norm_factors(nc, dve, g, p, b, step)
                if name == "final":
                    dve.wait_ge(hb_ready, b.times(1, 1))
                    if before(b, 2):
                        dve.wait_ge(stored[p], b.plus(-2).pairs(16))
                    nc.vector.scalar_tensor_tensor(out=z[p][:, :], in0=fin[p][:, :], scalar=g.a[p][:, :], in1=hb[p][:, :],
                                                   op0=ALU.mult, op1=ALU.add).then_inc(z_ready, 1)
            pipeline(dve, stages, do)


def padded_heads(w):
    t = np.zeros((2, 4, 32, w.shape[0]), w.dtype)
    t[:, :, :HD] = w.T.reshape(2, 4, HD, w.shape[0])
    return t.reshape(2, P, w.shape[0])


def matrices(i):
    m = {}
    q, k, v = np.split(i["L0_conv_qkv_w"], 3)
    m["a_q"], m["a_k"], m["a_v"] = q.T, k.T, v.T
    m["a_proj0"], m["a_proj1"] = padded_heads(i["L0_conv_proj_w"])
    for n in "qkv":
        m["c_" + n] = i["L2_conv_w" + n].T
    for h in range(2):
        m[f"c_dq{h}"], m[f"c_dk{h}"] = i[f"L2_conv_wq{h}"].T, i[f"L2_conv_wk{h}"].T
    m["c_vd"] = np.concatenate([i["L2_conv_wv0"].T, i["L2_conv_wv1"].T], 1)
    m["c_ff0"], m["c_ff1"] = padded_heads(i["L2_conv_ff_w1"][:, :P])
    m["c_ff2"] = i["L2_conv_ff_w1"][:, P:].T
    m["c_w2"], m["c_out"] = i["L2_conv_ff_w2"].T, i["L2_conv_out_w"].T
    w1 = np.zeros((P, 3, 32), np.float32)
    w1[:, :, :16] = i["L2_conv_sa_w1"][:, :, 0, 0].T[:, None, :]
    m["c_s1"] = w1.reshape(P, 96)
    w2 = i["L2_conv_sa_w2"]
    for dy in range(3):
        t = np.zeros((3, 32, 32), np.float32)
        t[:, :16, :16] = w2[:, :, dy, :].transpose(2, 1, 0)
        m[f"c_s2{dy}"] = t.reshape(96, 32)
    s3 = np.zeros((2, 32, P), np.float32)
    s3[:, :16] = i["L2_conv_sa_w3"][0, :, 0, 0][:, None]
    m["c_s3"] = s3.reshape(64, P)
    for n in "qk":
        t = np.zeros((P, 64), np.float32)
        t[:, :16] = i["L3_conv_W" + n].T
        m["d_" + n] = t
    m["d_v"] = i["L3_conv_Wv"].T
    at = np.arange(P)
    m["ident"] = np.eye(P, dtype=np.float32)
    m["ones"] = np.ones((P, P), np.float32)
    m["spread"] = (at[:, None] == 32 * (at[None] // 32) + 16).astype(np.float32)
    m["mean4"] = ((at[:, None] // 4) == (at[None] // 4)).astype(np.float32) / 4
    m["block"] = ((at[:, None] // CG) == (at[None] // CG)).astype(np.float32)
    return m


def vectors(i):
    v = {}
    b = i["L0_conv_qkv_b"]
    v["a_qb"], v["a_kb"] = b[:P], b[P:2 * P]
    t = padded_heads(b[None, 2 * P:])
    v["a_vb0"], v["a_vb1"] = t[0, :, 0], t[1, :, 0]
    v["a_pb"] = i["L0_conv_proj_b"]
    for n in ("pre_g", "pre_b", "norm_g", "norm_b", "post_g", "post_b", "ff_b1", "ff_b2", "out_b"):
        v["c_" + n] = i["L2_conv_" + n]
    t = np.zeros((3, 32), np.float32)
    t[:, :16] = i["L2_conv_sa_b1"]
    v["c_s1b"] = t.reshape(96)
    t = np.zeros((2, 32), np.float32)
    t[:, :16] = i["L2_conv_sa_b2"]
    v["c_s2b"] = t.reshape(64)
    v["c_s3b"] = np.repeat(i["L2_conv_sa_b3"], P)
    for n in "qk":
        v[f"d_{n}b"] = np.concatenate([i["L3_conv_b" + n], np.zeros(48, np.float32)])
    v["d_vb"], v["d_gamma"] = i["L3_conv_bv"], np.repeat(i["L3_conv_gamma"], P)
    return v


def packed(named):
    where, at = {}, 0
    for n, a in named.items():
        a = a if a.ndim == 2 else a[:, None]
        where[n] = (a.shape[0], at, at + a.shape[1])
        at += a.shape[1]
    out = np.zeros((P, at), np.float32)
    for n, a in named.items():
        rows, first, last = where[n]
        out[:rows, first:last] = a if a.ndim == 2 else a[:, None]
    return out, where


def program(nc, x, style, pos, mats, vecs, at, vat, out, scratch):
    with ExitStack() as ctx:
        sb = lambda name, shape: ctx.enter_context(nc.sbuf_tensor(name, shape, F32))
        sem = lambda name: ctx.enter_context(nc.semaphore(name))
        wt, vt = sb("mats_sb", [P, mats.shape[1]]), sb("vecs_sb", [P, vecs.shape[1]])
        made = sb("made", [P, 16])
        zero = made[:, 0:1]
        a_qb, a_out = made[:, 1:2], made[:, 2:3]
        halves = [made[0:96, 3:4], made[0:64, 4:5], made[:, 5:6]]
        half_b1 = made[:, 6:7]
        mean = [made[:, 7:8], made[:, 8:9]]
        offset = made[:, 9:10]
        M = {n: wt[0:rows, a:b] for n, (rows, a, b) in at.items()}
        V = {n: vt[0:rows, a:b] for n, (rows, a, b) in vat.items()}
        bank_pairs = [ctx.enter_context(nc.psum_tensor(f"banks{i}", [P, 2, 512], F32))[:, :, :] for i in range(4)]
        shared = {"bank_pairs": bank_pairs, "zero": zero, "ident": M["ident"], "ones": M["ones"], "spread": M["spread"]}
        head_scale = float(P) ** -0.5

        constants_loaded, product_made, setup_made = sem("constants_loaded"), sem("product_made"), sem("setup_made")
        ps = bank_pairs[0][:, 0, :]
        with nc.Block() as block:
            @block.sync
            def _(sp):
                sp.dma_start(wt[:, :], mats).then_inc(constants_loaded, 16)
                sp.dma_start(vt[:, :], vecs).then_inc(constants_loaded, 16)

            @block.tensor
            def _(pe):
                pe.wait_ge(constants_loaded, 32)
                nc.tensor.matmul(ps[:, 0:1], M["a_proj0"], V["a_vb0"], start=True, stop=False)
                nc.tensor.matmul(ps[:, 0:1], M["a_proj1"], V["a_vb1"], start=False, stop=True).then_inc(product_made, 1)

            @block.vector
            def _(dve):
                nc.vector.memset(zero, 0.0).then_inc(setup_made, 1)
                dve.wait_ge(constants_loaded, 32)
                nc.vector.tensor_scalar(a_qb, V["a_qb"], head_scale, None, ALU.mult).then_inc(setup_made, 1)
                for dst, src in zip(halves + [half_b1], (V["c_s1b"], V["c_s2b"], V["c_s3b"], V["c_ff_b1"])):
                    nc.vector.tensor_scalar(dst, src, 0.5, None, ALU.mult).then_inc(setup_made, 1)
                dve.wait_ge(product_made, 1)
                nc.vector.tensor_tensor(a_out, ps[:, 0:1], V["a_pb"], ALU.add).then_inc(setup_made, 1)
                dve.wait_ge(setup_made, 7)

        with nc.cleanup_on_exit():
            attention(
                nc, "a", Plan([Group("S", 4, 0, 32), Group("S", 4, 4, 32)], True), shared,
                {"qk": [M["a_q"], M["a_k"]], "v": M["a_v"], "proj": [M["a_proj0"], M["a_proj1"]]},
                x, None, x, scratch["y0"], scratch["parts"], head_scale,
                {"qk": [a_qb, V["a_kb"]], "out": a_out}, "bias")
        with ExitStack() as inner:
            sb = lambda name, shape: inner.enter_context(nc.sbuf_tensor(name, shape, F32))
            covs = [sb("cov_content", [P, P])[:, :], sb("cov_style", [P, P])[:, :]]
            move = sb("move", [P, P])[:, :]
            with nc.cleanup_on_exit():
                statistics(nc, "s", shared, style, STYLES, mean[1], covs[1])
            with nc.cleanup_on_exit():
                statistics(nc, "b", shared, scratch["y0"], NB, mean[0], covs[0])
            with nc.cleanup_on_exit():
                whiten(nc, M, shared, mean, covs, move, offset)
            with nc.cleanup_on_exit():
                gate(nc, M, V, shared, halves + [V["c_s2b"]], move, offset, scratch["y0"], pos,
                     scratch["h"], scratch["sh"], scratch["se"])
        with nc.cleanup_on_exit():
            attention(
                nc, "c", Plan([Group("S", 4, 0, 32), Group("S", 4, 4, 32), Group("D", 2, 0, 64)], True), shared,
                {"qk": [M["c_q"], M["c_k"]], "v": M["c_v"], "dqk": [[M["c_dq0"], M["c_dq1"]], [M["c_dk0"], M["c_dk1"]]],
                 "vd": M["c_vd"], "proj": [M["c_ff0"], M["c_ff1"], M["c_ff2"]]},
                scratch["sh"], scratch["se"], None, scratch["ff"], scratch["parts"], float(HD) ** -0.5,
                {"qk": [0.0, 0.0], "dqk": [0.0, 0.0], "dscale": 0.5 * 64.0 ** -0.5}, "plain")
        with nc.cleanup_on_exit():
            feed_forward(nc, M, V, shared, half_b1, scratch["ff"], scratch["h"], scratch["z"])
        with nc.cleanup_on_exit():
            attention(
                nc, "d", Plan([Group("D", 1, 0, P)], False), shared,
                {"dqk": [[M["d_q"]], [M["d_k"]]], "vd": M["d_v"]},
                scratch["z"], None, scratch["z"], out, None, 1.0,
                {"dqk": [V["d_qb"], V["d_kb"]], "dscale": 1.0, "v": V["d_vb"], "gamma": V["d_gamma"]}, "gamma")


def kernel(**inputs):
    import concourse.bacc as _bacc
    from concourse.bass_utils import run_bass_kernel_spmd as _run

    i = {name: np.asarray(a) for name, a in inputs.items()}
    mats, mats_at = packed(matrices(i))
    vecs, vecs_at = packed(vectors(i))
    arrays = {
        "in_x": np.ascontiguousarray(i["x"]).reshape(NB, P, N),
        "in_style": np.ascontiguousarray(i["L1_conv_s_B"]).reshape(STYLES, P, N),
        "in_pos": np.ascontiguousarray(i["L2_conv_pos_emb"]).reshape(P, N),
        "in_mats": mats, "in_vecs": vecs,
    }
    nc = _bacc.Bacc("TRN2", target_bir_lowering=False, num_devices=1)
    given = [nc.dram_tensor(n, a.shape, F32, kind="ExternalInput").ap() for n, a in arrays.items()]
    out = nc.dram_tensor("out_image", (NB, P, N), F32, kind="ExternalOutput").ap()
    between = lambda name, shape, dt: nc.dram_tensor(name, shape, dt, kind="Internal").ap()
    scratch = {name: between(name, (NB, P, N), F32) for name in ("y0", "h", "sh", "se", "ff", "z")}
    scratch["parts"] = [between(name, (3, P, N), BF16) for name in ("q_parts", "k_parts")]
    program(nc, *given, mats_at, vecs_at, out, scratch)
    r = _run(nc, [arrays], core_ids=[0])
    return r.results[0]["out_image"].reshape(NB, P, SIDE, SIDE)
```

```python
from contextlib import ExitStack

import numpy as np

import concourse.bass as bass
from concourse import mybir

F32, BF16 = mybir.dt.float32, mybir.dt.bfloat16
ACT, ALU, AX = mybir.ActivationFunctionType, mybir.AluOpType, mybir.AxisListType

P = 128
NB = 16
SIDE = 32
N = SIDE * SIDE
KC = N // P
HEADS, HD = 8, P // 8
STYLES = 4
CG = 16
EPS_COV, EPS_GN = 0.01, 1e-6
ROOT_STEPS = 24
TERMS = [(0, 0), (0, 1), (1, 0), (0, 2), (2, 0), (1, 1)]
SROWS = 16 * len(TERMS) + 2
BANKS = 3


class Batch:

    def __init__(self, k, p):
        self.k, self.p = k, p

    def plus(self, n):
        return Batch(self.k, self.p + n)

    def times(self, n, c=0):
        return self.k * (2 * n) + (n * self.p + c)

    def pairs(self, n):
        return self.k * n + (self.p // 2 + 1) * n

    @property
    def parity(self):
        return self.p % 2

    def index(self):
        return (self.k * 2 + self.p) % NB


def some(value):
    return not (isinstance(value, int) and value <= 0)


def cuts(steps, n):
    return [steps[len(steps) * i // n:len(steps) * (i + 1) // n] for i in range(n)]


def alternate(few, many):
    n = min(len(few), len(many))
    return [s for pair in zip(few, many) for s in pair] + few[n:] + many[n:]


class Group:

    def __init__(self, kind, heads, first, width):
        self.kind, self.heads, self.first, self.width = kind, heads, first, width
        self.narrow = width == 32


class Plan:

    def __init__(self, groups, proj, order):
        self.groups, self.proj, self.order = groups, proj, order
        self.s_groups = [g for g, x in enumerate(groups) if x.kind == "S"]
        self.d_group = next((g for g, x in enumerate(groups) if x.kind == "D"), None)
        self.wide_group = next((g for g, x in enumerate(groups) if not x.narrow), None)
        self.mixed = self.d_group is not None
        self.single = len(groups) == 1
        self.tiles = 1 if self.single else 2
        self.units = sum(g.heads * KC for g in groups)
        self.quads = KC * len(groups)
        self.maxes = sum(g.heads * KC * 2 for g in groups)
        self.d_heads = groups[self.d_group].heads if self.d_group is not None else 0
        self.wide_heads = groups[self.wide_group].heads if self.wide_group is not None else 0
        self.prologue = self.load_steps(0) + self.max_steps(0, 0) + [("turn", 0, 0)] + self.scores(0, 0, 0) + self.early(0, 0)
        self.first = self.image(False, True)
        self.usual = self.image(True, True)
        self.nearly = self.image(True, True, far=False)
        self.last = self.image(True, False)
        self.epilogue = self.tail(0)

    LATE, EARLY = 14, 12

    def qk_steps(self, b):
        return [("qk", b, t) for t in range(2 * self.tiles)] + [("split", b)]

    def dqk_steps(self, b):
        return [("dqk", b, w, h, half) for w in range(2) for h in range(self.d_heads) for half in range(2)]

    def v_steps(self, b):
        s = [("v", b, t) for t in range(2)] if any(g.narrow for g in self.groups) else []
        return s + ([("vd", b, t) for t in range(2)] if self.wide_heads else [])

    def load_steps(self, b):
        out = [("load", b)] + self.qk_steps(b) + [("stack", b)] + self.v_steps(b)
        if self.single:
            out += [("load", b + 1)] + self.qk_steps(b + 1) + [("stack", b + 1)]
        elif not self.mixed:
            out += [("load", b + 1)]
        return out

    def make_steps(self, g, ahead, far, maxes):
        last = g == len(self.groups) - 1
        if self.single:
            if not ahead:
                return maxes
            cut = len(maxes) // 2
            load, qk = ([("load", 2)], self.qk_steps(2)) if far else ([], [])
            return self.v_steps(1) + load + maxes[:cut] + qk + maxes[cut:]
        out = []
        if self.mixed and g == 0:
            out += self.dqk_steps(0) + [("load", 1)]
        if ahead and g == (1 if self.mixed else 0):
            out += self.qk_steps(1) + [("stack", 1)]
        if ahead and last:
            out += self.v_steps(1) + ([] if self.mixed else [("load", 2)])
        return alternate(out, maxes)

    def max_steps(self, b, g):
        return [("max", b, g, h, qc, half) for h in range(self.groups[g].heads) for qc in range(KC) for half in range(2)]

    def after(self, b, g):
        return (b, g + 1) if g + 1 < len(self.groups) else (b + 1, 0)

    def early(self, b, g):
        steps = self.max_steps(*self.after(b, g))
        return steps[:len(steps) // 6] if len(self.groups) > 1 else []

    def tail(self, b):
        g = len(self.groups) - 1
        return [("sums", b, g), ("norm", b, g, 0), ("norm", b, g, 1)] + self.finish(b)

    def with_norms(self, b, g, maxes):
        norm = [("norm", b, g, half) for half in range(2)]
        return maxes[:3] + [("sums", b, g)] + maxes[3:5] + norm[:1] + maxes[5:6] + norm[1:] + maxes[6:]

    def finish(self, b):
        return [("proj", b, 0), ("proj", b, 1), ("store", b), ("residual", b + 1)]

    def scores(self, b, g, kc):
        return [("scores", b, g, kc, h) for h in range(self.groups[g].heads)]

    def image(self, tail, ahead, far=True):
        out = []
        n = len(self.groups)
        for g in range(n):
            last = g == n - 1
            nb, ng = self.after(0, g)
            there = ahead or not last
            maxes = self.max_steps(nb, ng)[len(self.early(0, g)):] if there else []
            if g > 0:
                maxes = self.with_norms(0, g - 1, maxes)
            elif tail:
                maxes = self.with_norms(-1, n - 1, maxes)
                cut = min(len(maxes), 26)
                maxes = maxes[:cut] + self.finish(-1) + maxes[cut:]
            work = self.make_steps(g, ahead, far, maxes)
            turn = [("turn", nb, ng)] if there else []
            share = cuts(work, 8 * (KC - 1))
            if self.single:
                share = [work[:2]] + [[]] * self.LATE + cuts(work[2:], 8 * (KC - 1) - self.LATE - 2 - self.EARLY) + [turn] + [[]] * self.EARLY
            for kc in range(KC):
                pv = [("pv", 0, g, kc, half) for half in range(2)]
                if kc < KC - 1:
                    nxt = cuts(self.scores(0, g, kc + 1), 4)
                    a = share[8 * kc:8 * kc + 8]
                    pieces = {"s": nxt, "w": a, "p": [pv[:1], pv[1:]]}
                    for kind in self.order:
                        out += pieces[kind].pop(0)
                else:
                    begun = there and (ahead or self.after(nb, ng)[0] == 0)
                    a = cuts(self.early(nb, ng) if begun else [], 8)
                    nxt = cuts(self.scores(nb, ng, 0) if there else [], 4)
                    out += pv[:1] + ([] if self.single else turn) + a[0] + a[1] + a[2] + a[3] + pv[1:] + [("evacuate", 0, g)]
                    out += [("stack", 2)] if self.single and ahead and far else []
                    out += a[4] + nxt[0] + a[5] + nxt[1] + a[6] + nxt[2] + a[7] + nxt[3]
        return out

    BANKED = ("qk", "dqk", "v", "vd", "max", "turn", "sums", "norm", "proj")

    def banked(self, steps):
        return [s for s in steps if self.is_banked(s)]

    def is_banked(self, step):
        return step[0] in self.BANKED and (self.proj or step[0] != "proj")

    def bank_of(self, section, i):
        bank = i % BANKS
        fills = lambda steps: len(range(bank, len(self.banked(steps)), BANKS))
        pro, first, usual, nearly, last = (fills(x) for x in (self.prologue, self.first, self.usual, self.nearly, self.last))
        now = i // BANKS + 1
        where, p = section
        if where == "prologue":
            return bank, 0, now
        if where == "loop":
            return bank, 2 * usual, pro + first + (p - 1) * usual + now
        if where == "peeled" and p < NB - 1:
            return bank, 0, pro + (first + (p - 1) * usual if p else 0) + now
        before_last = pro + first + (NB - 3) * usual + nearly
        return bank, 0, before_last + (last if where == "epilogue" else 0) + now

    def half_before(self, u):
        halves = 2 * self.units
        return u - BANKS if u >= BANKS else max(x for x in range(halves) if x % BANKS == u) - halves

    def unit(self, g, kc, h):
        return sum(x.heads * KC for x in self.groups[:g]) + kc * self.groups[g].heads + h

    def quad(self, g, kc):
        return g * KC + kc

    def max_number(self, g, h, qc, half):
        return sum(x.heads * KC * 2 for x in self.groups[:g]) + (h * KC + qc) * 2 + half


def walk(eng, plan, do):

    def section(steps, image, where):
        n = 0
        for step in steps:
            bank = None
            if plan.is_banked(step):
                at, slope, const = plan.bank_of(where, n)
                bank = (at, image.k * slope + const if slope else const)
                n += 1
            do(step, image, bank)

    section(plan.prologue, Batch(0, 0), ("prologue", 0))
    section(plan.first, Batch(0, 0), ("peeled", 0))
    section(plan.usual, Batch(0, 1), ("peeled", 1))
    with eng.Fori(1, NB // 2 - 1) as k:
        section(plan.usual, Batch(k, 0), ("loop", 0))
        section(plan.usual, Batch(k, 1), ("loop", 1))
    section(plan.nearly, Batch(NB // 2 - 1, 0), ("peeled", NB - 2))
    section(plan.last, Batch(NB // 2 - 1, 1), ("peeled", NB - 1))
    section(plan.epilogue, Batch(NB // 2 - 1, 1), ("epilogue", 0))


def attention(nc, tag, plan, shared, W, x_in, xe_in, res_in, out, scratch, scale_q, bias, final):
    G = plan.groups
    zero, ident, ones, pick = (shared[n] for n in ("zero", "ident", "ones", "pick"))
    S = bool(plan.s_groups)
    D, WIDE, narrow = plan.d_heads, plan.wide_heads, any(g.narrow for g in G)
    s_heads = sum(G[g].heads for g in plan.s_groups)
    rows_q = HD * s_heads
    with ExitStack() as ctx:
        sb = lambda name, shape, dt: ctx.enter_context(nc.sbuf_tensor(f"{tag}_{name}", shape, dt))
        sem = lambda name: nc.alloc_semaphore(f"{tag}_{name}")
        pairs = shared["bank_pairs"]
        st = [pairs[0][:, 0, :], pairs[0][:, 1, :], pairs[1][:, 0, :]]
        po = pairs[2]
        bk = [pairs[1][:, 1, :], pairs[3][:, 0, :], pairs[3][:, 1, :]]

        xin = sb("xin", [P, N], F32)
        xe = sb("xe", [P, N], F32) if xe_in is not None else xin
        if S:
            qkf = sb("qkf", [P, plan.tiles, N], F32)
            parts = [sb(f"parts{w}", [P, 3, N], BF16) for w in range(plan.tiles)]
            stack = [[sb(f"stack{w}{p}", [SROWS, s_heads, N], BF16) for p in range(2)] for w in range(2)]
            top = sb("top", [P, P], BF16)
            low = sb("low", [P, P], BF16)
        if narrow:
            vs = [sb(f"vs{p}", [P, KC, s_heads, 32], F32) for p in range(2)]
        if D:
            dq = [[sb(f"dqk{w}", [65, D, N], F32)] * 2 for w in range(2)]
            turned = sb("turned", [P, P], F32)
        if WIDE:
            vd = [sb(f"vd{p}", [P, KC, P], F32) for p in range(2)]
            esum = [sb(f"esum{p}", [P, WIDE, N], F32) for p in range(1 if D else 2)] * (2 if D else 1)
        ring = max(g.heads for g in G)
        rounds = 4 if plan.single else 2
        e = [sb(f"e{i}", [P, ring, N], F32) for i in range(rounds)]
        osb = [sb(f"osb{g}", [P, N], F32) for g in range(len(G))]
        inverse = sb("inverse", [P, KC * ring], F32)
        wide = sb("wide", [P, N], F32)
        y = sb("y", [P, N], F32)
        res = sb("res", [P, N], F32) if res_in is not None else None
        mx = sb("mx", [P, ring * KC, 2], F32)
        negm = sb("negm", [P, P], F32)

        const_ready = sem("const_ready")
        x_loaded = sem("x_loaded")
        res_loaded = sem("res_loaded")
        first_part = sem("first_part")
        qk_evacuated = sem("qk_evacuated")
        split_step = sem("split_step")
        q_split = sem("q_split")
        parts_stored = sem("parts_stored")
        stack_ready = sem("stack_ready")
        dqk_ready = sem("dqk_ready")
        v_ready = sem("v_ready")
        max_done = sem("max_done")
        negmax_ready = sem("negmax_ready")
        top_ready = sem("top_ready")
        turned_ready = sem("turned_ready")
        smax_ready = sem("smax_ready")
        dmax_ready = sem("dmax_ready")
        scores_ready = sem("scores_ready")
        exp_done = sem("exp_done")
        esum_done = sem("esum_done")
        pv_done = sem("pv_done")
        out_ready = sem("out_ready")
        evacuated = sem("evacuated")
        bank_full = [sem(f"bank_full{i}") for i in range(BANKS)]
        bank_free = [sem(f"bank_free{i}") for i in range(BANKS)]
        inverse_ready = sem("inverse_ready")
        wide_ready = sem("wide_ready")
        norm_done = sem("norm_done")
        y_step = sem("y_step")
        y_ready = sem("y_ready")
        stored = sem("stored")
        block = ctx.enter_context(nc.Block())

        n_g = len(G)
        split_rows = slice(0, P if plan.tiles == 2 else 64)
        n_norm = 2 * n_g
        n_vs = 2 * narrow + 2 * bool(WIDE)
        n_loads = 2 if xe_in is not None else 1
        n_dqk = 4 * D
        n_const = 2 + 4 * narrow + bool(D) + 1

        def skip(b):
            return isinstance(b.k, int) and 2 * b.k + b.p >= NB

        def since(image, rel):
            return not (isinstance(image.k, int) and 2 * image.k + image.p + rel < 0)

        @block.sync
        def _(sp):
            def do(step, image, bank):
                kind, b = step[0], image.plus(step[1])
                if kind in ("load", "residual", "store") and not isinstance(b.k, int):
                    row = sp.snap(b.index())
                else:
                    row = b.index()
                if kind == "load":
                    if skip(b):
                        return
                    if since(b, -1) and plan.mixed:
                        sp.wait_ge(dqk_ready, b.times(n_dqk))
                    elif since(b, -1):
                        sp.wait_ge(v_ready, b.times(n_vs))
                    sp.dma_start(xin[:, :], x_in[row]).then_inc(x_loaded, 16)
                    if xe_in is not None:
                        sp.dma_start(xe[:, :], xe_in[row]).then_inc(x_loaded, 16)
                if kind == "residual" and res is not None and not skip(b):
                    if since(b, -1):
                        sp.wait_ge(y_ready, b.times(2))
                    sp.dma_start(res[:, :], res_in[row]).then_inc(res_loaded, 16)
                if kind == "stack":
                    for w in range(2):
                        tile = parts[w] if plan.tiles == 2 else parts[0][32 * w:32 * w + HD]
                        if w < plan.tiles:
                            sp.wait_ge(q_split, b.times(plan.tiles, 1 + w))
                        elif since(b, -2):
                            sp.wait_ge(scores_ready, b.plus(-1).times(2 * plan.units))
                        sp.dma_start(scratch[w][:, 0:rows_q, :].rearrange("t p n -> p t n"), tile[:, :, :]).then_inc(parts_stored, 16)
                    sp.wait_ge(parts_stored, b.times(32, 32))
                    for w in range(2):
                        for t in range(6):
                            src = scratch[w][TERMS[t][w], 0:rows_q, :].rearrange("(h d) n -> d h n", d=16)
                            sp.dma_start(stack[w][b.parity][16 * t:16 * t + 16, :, :], src).then_inc(stack_ready, 16)
                if kind == "turn":
                    g = step[2]
                    sp.wait_ge(turned_ready, b.times(n_g, g + 1))
                    h0, rows = G[g].first, G[g].heads * KC
                    if G[g].kind == "S":
                        for row, part in ((96, top), (97, low)):
                            sp.dma_start(stack[0][b.parity][row:row + 1, h0:h0 + G[g].heads, :],
                                         part[0:rows, :]).then_inc(smax_ready, 16)
                    else:
                        sp.dma_start(dq[0][b.parity][64:65, :, :], turned[0:rows, :]).then_inc(dmax_ready, 16)
                if kind == "store":
                    sp.wait_ge(y_ready, b.times(2, 2))
                    sp.dma_start(out[row], y[:, :]).then_inc(stored, 16)

            if res is not None:
                sp.dma_start(res[:, :], res_in[0]).then_inc(res_loaded, 16)
            walk(sp, plan, do)
            sp.wait_ge(stored, 16 * NB)

        @block.gpsimd
        def _(pool):
            def do(step, image, bank):
                kind, b = step[0], image.plus(step[1])
                if kind == "split":
                    for w in range(plan.tiles):
                        src, dst = qkf[split_rows, w, :], parts[w][split_rows]
                        nought = zero[split_rows, 0:1].to_broadcast([split_rows.stop, N])
                        pool.wait_ge(qk_evacuated, b.times(2 * plan.tiles, 2 + 2 * w))
                        if since(b, -1):
                            pool.wait_ge(parts_stored, b.times(32))
                        nc.gpsimd.tensor_tensor(src, src, dst[:, 0, :], ALU.subtract).then_inc(split_step, 1)
                        pool.wait_ge(split_step, b.times(2 * plan.tiles, 2 * w + 1))
                        nc.gpsimd.tensor_tensor(dst[:, 1, :], src, nought, ALU.add).then_inc(split_step, 1)
                        pool.wait_ge(split_step, b.times(2 * plan.tiles, 2 * w + 2))
                        nc.gpsimd.tensor_tensor(dst[:, 2, :], src, dst[:, 1, :], ALU.subtract).then_inc(q_split, 1)
                if kind == "scores" and not G[step[2]].narrow:
                    g, kc, h = step[2:]
                    pool.wait_ge(exp_done, b.times(2 * plan.units, 2 * plan.unit(g, kc, h) + 2))
                    src = e[plan.quad(g, kc) % rounds][:, h, :]
                    if kc == 0:
                        ago = 1 if D else 2
                        if since(b, -ago):
                            pool.wait_ge(inverse_ready, b.plus(1 - ago).times(n_g))
                        nc.gpsimd.tensor_tensor(esum[b.parity][:, h, :], src, zero[:, 0:1].to_broadcast([P, N]), ALU.add).then_inc(esum_done, 1)
                    else:
                        pool.wait_ge(esum_done, b.times(KC * WIDE, (kc - 1) * WIDE + h + 1))
                        nc.gpsimd.tensor_tensor(esum[b.parity][:, h, :], src, esum[b.parity][:, h, :], ALU.add).then_inc(esum_done, 1)

            walk(pool, plan, do)

        @block.tensor
        def _(pe):
            half_of = lambda t, half: t[:, 512 * half:512 * half + 512]

            def do(step, image, bank):
                kind, b = step[0], image.plus(step[1])
                p = b.parity
                if bank is not None:
                    dst, full = bk[bank[0]], bank_full[bank[0]]
                    if not (isinstance(bank[1], int) and bank[1] < 2):
                        pe.wait_ge(bank_free[bank[0]], bank[1] - 1)
                if kind == "qk":
                    t = step[2]
                    if t == 0:
                        pe.wait_ge(x_loaded, b.times(16 * n_loads, 16 * n_loads))
                    nc.tensor.matmul(dst[split_rows, :], W["qk"][t // 2], half_of(xin, t % 2), start=True, stop=True).then_inc(full, 1)
                if kind == "dqk":
                    w, h, half = step[2:]
                    nc.tensor.matmul(dst[0:64, :], W["dqk"][w][h], half_of(xe if w == 0 else xin, half),
                                     start=True, stop=True).then_inc(full, 1)
                if kind in ("v", "vd"):
                    for c in range(4):
                        kc = 4 * step[2] + c
                        mm = nc.tensor.matmul(dst[:, P * c:P * c + P], xin[:, P * kc:P * kc + P], W[kind],
                                              start=True, stop=True)
                    mm.then_inc(full, 1)
                if kind == "max":
                    g, h, qc, half = step[2:]
                    if (h, qc, half) == (0, 0, 0):
                        if G[g].kind == "S":
                            pe.wait_ge(stack_ready, b.times(192, 192))
                        else:
                            pe.wait_ge(dqk_ready, b.times(n_dqk, n_dqk))
                    if G[g].kind == "S":
                        ah = G[g].first + h
                        lhs, rhs = stack[0][p][0:96, ah, P * qc:P * qc + P], stack[1][p][0:96, ah, 512 * half:512 * half + 512]
                    else:
                        lhs, rhs = dq[0][p][0:64, h, P * qc:P * qc + P], dq[1][p][0:64, h, 512 * half:512 * half + 512]
                    nc.tensor.matmul(dst[:, :], lhs, rhs, start=True, stop=True).then_inc(full, 1)
                if kind == "turn":
                    pe.wait_ge(negmax_ready, b.times(n_g, step[2] + 1))
                    nc.tensor.transpose(dst[:, 0:P], negm[:, :], ident[:, :]).then_inc(full, 1)
                if kind == "scores":
                    g, kc, h = step[2:]
                    u = plan.unit(g, kc, h)
                    if (kc, h) == (0, 0):
                        if G[g].kind == "S":
                            n_s = len(plan.s_groups)
                            pe.wait_ge(smax_ready, b.times(32 * n_s, 32 * (g + 1)))
                        else:
                            pe.wait_ge(dmax_ready, b.times(16, 16))
                            pe.wait_ge(const_ready, n_const)
                    for half in range(2):
                        before_u = plan.half_before(2 * u + half)
                        if before_u >= 0 or since(b, -1):
                            pe.wait_ge(exp_done, b.times(2 * plan.units, before_u + 1))
                        if G[g].kind == "S":
                            ah = G[g].first + h
                            lhs, rhs = stack[1][p][:, ah, P * kc:P * kc + P], stack[0][p][:, ah, 512 * half:512 * half + 512]
                        else:
                            lhs, rhs = dq[1][p][:, h, P * kc:P * kc + P], dq[0][p][:, h, 512 * half:512 * half + 512]
                        nc.tensor.matmul(st[(2 * u + half) % BANKS], lhs, rhs, start=True, stop=True).then_inc(scores_ready, 1)
                if kind == "pv":
                    g, kc, half = step[2:]
                    if half == 0:
                        pe.wait_ge(exp_done, b.times(2 * plan.units, 2 * plan.unit(g, kc, G[g].heads - 1) + 2))
                        if kc == 0:
                            if g == 0:
                                pe.wait_ge(v_ready, b.times(n_vs, n_vs))
                            if g or since(b, -1):
                                pe.wait_ge(evacuated, b.times(n_g, g))
                    for h in range(G[g].heads):
                        src = e[plan.quad(g, kc) % rounds][:, h, 512 * half:512 * half + 512]
                        width = G[g].width
                        v = vs[p][:, kc, G[g].first + h, :] if G[g].narrow else vd[p][:, kc, width * h:width * h + width]
                        mm = nc.tensor.matmul(po[width * h:width * h + width, half, :], v, src,
                                              start=(kc == 0), stop=(kc == KC - 1), skip_group_check=True,
                                              tile_position=(0, width * h) if width < P else None)
                    if half == 1:
                        mm.then_inc(pv_done, 1)
                if kind == "sums":
                    g, heads = step[2], G[step[2]].heads
                    if G[g].narrow:
                        pe.wait_ge(evacuated, b.times(n_g, g + 1))
                    else:
                        pe.wait_ge(esum_done, b.times(KC * WIDE, KC * WIDE))
                    for c in range(KC):
                        if G[g].narrow:
                            mm = nc.tensor.matmul(dst[:, heads * c:heads * c + heads], osb[g][:, P * c:P * c + P], pick, start=True, stop=True)
                        else:
                            for h in range(heads):
                                mm = nc.tensor.matmul(dst[:, heads * c + h:heads * c + h + 1], esum[p][:, h, P * c:P * c + P],
                                                      ones[:, 0:1], start=True, stop=True)
                    mm.then_inc(full, 1)
                if kind == "norm":
                    g, half = step[2:]
                    if half == 0:
                        pe.wait_ge(wide_ready, b.times(n_g, g + 1))
                    for c in range(4):
                        at = P * (4 * half + c)
                        mm = nc.tensor.matmul(dst[:, P * c:P * c + P], wide[:, at:at + P], ident[:, :], start=True, stop=True)
                    mm.then_inc(full, 1)
                if kind == "proj" and final != "gamma":
                    half = step[2]
                    pe.wait_ge(norm_done, b.times(n_norm, n_norm))
                    for g in range(n_g):
                        mm = nc.tensor.matmul(dst[:, :], W["proj"][g], half_of(osb[g], half), start=(g == 0), stop=(g == n_g - 1))
                    mm.then_inc(full, 1)

            pe.wait_ge(const_ready, n_const)
            walk(pe, plan, do)

        @block.scalar
        def _(act):
            def do(step, image, bank):
                kind, b = step[0], image.plus(step[1])
                p = b.parity
                if kind == "qk":
                    t = step[2]
                    act.wait_ge(bank_full[bank[0]], bank[1])
                    w, cut = t // 2, slice(512 * (t % 2), 512 * (t % 2) + 512)
                    if since(b, -1):
                        act.wait_ge(q_split, b.times(plan.tiles, w + 1 - plan.tiles))
                        act.wait_ge(parts_stored, b.times(32))
                    src, how = bk[bank[0]][split_rows, :], dict(bias=bias["qk"][w], scale=scale_q if w == 0 else 1.0)
                    nc.scalar.activation(parts[w][split_rows, 0, cut], src, ACT.Identity, **how).then_inc(first_part, 1)
                    nc.scalar.activation(qkf[split_rows, w, cut], src, ACT.Identity, **how).then_inc(bank_free[bank[0]], 1)
                    act.wait_ge(first_part, b.times(2 * plan.tiles, t + 1))
                    act.wait_ge(bank_free[bank[0]], bank[1])
                    act.sem_inc(qk_evacuated, 1)
                if kind == "dqk":
                    w, h, half = step[2:]
                    act.wait_ge(bank_full[bank[0]], bank[1])
                    nc.scalar.activation(dq[w][p][0:64, h, 512 * half:512 * half + 512], bk[bank[0]][0:64, :], ACT.Identity,
                                         bias=bias["dqk"][w], scale=bias["dscale"] if w == 0 else 1.0).then_inc(bank_free[bank[0]], 1)
                    act.wait_ge(bank_free[bank[0]], bank[1])
                    act.sem_inc(dqk_ready, 1)
                if kind == "scores":
                    g, kc, h = step[2:]
                    u = plan.unit(g, kc, h)
                    q = plan.quad(g, kc)
                    if h == 0 and not (isinstance(b.k, int) and 2 * b.k + b.p == 0 and q < rounds):
                        act.wait_ge(pv_done, b.times(plan.quads, q + 1 - rounds))
                        if WIDE and (not G[g].narrow or g == 0):
                            added = b.times(KC * WIDE, (kc + 1 - rounds) * WIDE)
                            if (not G[g].narrow or kc < 2) and some(added):
                                act.wait_ge(esum_done, added)
                    for half in range(2):
                        act.wait_ge(scores_ready, b.times(2 * plan.units, 2 * u + half + 1))
                        nc.scalar.activation(e[q % rounds][:, h, 512 * half:512 * half + 512], st[(2 * u + half) % BANKS],
                                             ACT.Exp).then_inc(exp_done, 1)
                if kind == "evacuate":
                    g = step[2]
                    act.wait_ge(pv_done, b.times(plan.quads, plan.quad(g, KC - 1) + 1))
                    if since(b, -1):
                        act.wait_ge(y_ready, b.times(2))
                    nc.scalar.activation(osb[g][:, :], po[:, :, :].rearrange("p a b -> p (a b)"), ACT.Copy).then_inc(evacuated, 1)
                if kind == "sums":
                    g = step[2]
                    act.wait_ge(inverse_ready, b.times(n_g, g + 1))
                    if g or since(b, -1):
                        act.wait_ge(norm_done, b.times(n_norm, 2 * g))
                    heads, width = G[g].heads, G[g].width
                    src = inverse[:, 0:KC * heads].unsqueeze(2).to_broadcast([P, KC * heads, width])
                    nc.scalar.activation(wide[:, :].rearrange("p (a w) -> p a w", w=width), src, ACT.Copy).then_inc(wide_ready, 1)

            walk(act, plan, do)

        @block.vector
        def _(dve):
            def do(step, image, bank):
                kind, b = step[0], image.plus(step[1])
                p = b.parity
                if bank is not None and kind in ("v", "vd", "max", "turn", "sums", "norm", "proj"):
                    src, free = bk[bank[0]], bank_free[bank[0]]
                    dve.wait_ge(bank_full[bank[0]], bank[1])
                if kind in ("v", "vd"):
                    t = step[2]
                    if t == 0 and since(b, -2):
                        dve.wait_ge(pv_done, b.plus(-1).times(plan.quads))
                    if kind == "v":
                        nc.vector.tensor_copy(vs[p][:, 4 * t:4 * t + 4, :, 0:16],
                                              src[:, :].rearrange("p (c h d) -> p c h d", c=4, d=16)).then_inc(free, 1)
                    else:
                        nc.vector.tensor_copy(vd[p][:, 4 * t:4 * t + 4, :],
                                              src[:, :].rearrange("p (c m) -> p c m", c=4)).then_inc(free, 1)
                    dve.wait_ge(free, bank[1])
                    dve.sem_inc(v_ready, 1)
                if kind == "max":
                    g, h, qc, half = step[2:]
                    if (h, qc, half) == (0, 0, 0) and (g or since(b, -1)):
                        dve.wait_ge(negmax_ready, b.times(n_g, g))
                    nc.vector.tensor_reduce(mx[:, h * KC + qc, half:half + 1], src[:, :], AX.X, ALU.max).then_inc(free, 1)
                    if (h, qc, half) == (G[g].heads - 1, KC - 1, 1):
                        dve.wait_ge(free, bank[1])
                        if g or since(b, -1):
                            dve.wait_ge(turned_ready, b.times(n_g, g))
                        rows = G[g].heads * KC
                        nc.vector.tensor_reduce(negm[:, 0:rows], mx[:, 0:rows, :], AX.X, ALU.max, negate=True).then_inc(negmax_ready, 1)
                if kind == "turn":
                    g = step[2]
                    if G[g].kind == "S":
                        n_s = len(plan.s_groups)
                        if g or since(b, -1):
                            dve.wait_ge(smax_ready, b.times(32 * n_s, 32 * g))
                        nc.vector.tensor_copy(top[:, :], src[:, 0:P]).then_inc(top_ready, 1)
                        dve.wait_ge(top_ready, b.times(n_s, g + 1))
                        nc.vector.tensor_tensor(low[:, :], src[:, 0:P], top[:, :], ALU.subtract).then_inc(free, 1)
                    else:
                        if since(b, -1):
                            dve.wait_ge(dmax_ready, b.times(16))
                        nc.vector.tensor_copy(turned[:, :], src[:, 0:P]).then_inc(free, 1)
                    dve.wait_ge(free, bank[1])
                    dve.sem_inc(turned_ready, 1)
                if kind == "sums":
                    g = step[2]
                    if g or since(b, -1):
                        dve.wait_ge(wide_ready, b.times(n_g, g))
                    nc.vector.reciprocal(inverse[:, 0:KC * G[g].heads], src[:, 0:KC * G[g].heads]).then_inc(free, 1)
                    dve.wait_ge(free, bank[1])
                    dve.sem_inc(inverse_ready, 1)
                if kind == "norm":
                    g, half = step[2:]
                    cut = slice(512 * half, 512 * half + 512)
                    if not G[g].narrow:
                        dve.wait_ge(evacuated, b.times(n_g, g + 1))
                    nc.vector.tensor_tensor(osb[g][:, cut], src[:, :], osb[g][:, cut], ALU.mult).then_inc(free, 1)
                    dve.wait_ge(free, bank[1])
                    dve.sem_inc(norm_done, 1)
                if kind == "proj":
                    half = step[2]
                    cut = slice(512 * half, 512 * half + 512)
                    if half == 0:
                        if since(b, -1):
                            dve.wait_ge(stored, b.times(16))
                        if res is not None:
                            dve.wait_ge(res_loaded, b.times(16, 16))
                    if final == "bias":
                        nc.vector.scalar_tensor_tensor(out=y[:, cut], in0=src[:, :], scalar=bias["out"], in1=res[:, cut],
                                                       op0=ALU.add, op1=ALU.add).then_inc(free, 1)
                    elif final == "plain":
                        nc.vector.tensor_copy(y[:, cut], src[:, :]).then_inc(free, 1)
                    else:
                        dve.wait_ge(norm_done, b.times(n_norm, half + 1))
                        nc.vector.tensor_scalar(osb[0][:, cut], osb[0][:, cut], bias["v"], bias["gamma"], ALU.add, ALU.mult).then_inc(y_step, 1)
                        dve.wait_ge(y_step, b.times(2, half + 1))
                        nc.vector.tensor_tensor(y[:, cut], osb[0][:, cut], res[:, cut], ALU.add).then_inc(y_ready, 1)
                    if final != "gamma":
                        dve.wait_ge(free, bank[1])
                        dve.sem_inc(y_ready, 1)

            for p in range(2):
                nc.vector.memset(stack[1][p][96:98, :, :], 1.0).then_inc(const_ready, 1)
            if narrow:
                for p in range(2):
                    nc.vector.memset(vs[p][:, :, :, 16:32], 0.0).then_inc(const_ready, 1)
                dve.wait_ge(const_ready, 4)
                for p in range(2):
                    nc.vector.memset(vs[p][:, :, :, 16:17], 1.0).then_inc(const_ready, 1)
            if D:
                nc.vector.memset(dq[1][0][64:65, :, :], 1.0).then_inc(const_ready, 1)
            nc.vector.memset(negm[:, :], 0.0).then_inc(const_ready, 1)

            walk(dve, plan, do)


def pipeline(eng, stages, do, images=NB):
    lag = max(x for _, x in stages)

    def turn(k, p):
        for name, late in stages:
            b = Batch(k, p - late)
            if isinstance(k, int) and not 0 <= 2 * k + b.p < images:
                continue
            do(name, b)

    whole = min((lag + 3) // 2 * 2, images)
    for t in range(whole):
        turn(t // 2, t % 2)
    if whole < images:
        with eng.Fori(whole // 2, images // 2) as k:
            turn(k, 0)
            turn(k, 1)
    for t in range(images, images + lag):
        turn(t // 2, t % 2)


def before(b, n=1):
    return not (isinstance(b.k, int) and 2 * b.k + b.p - n < 0)


def statistics(nc, tag, shared, x_in, images, mean, cov):
    with ExitStack() as ctx:
        sb = lambda name, shape: ctx.enter_context(nc.sbuf_tensor(f"{tag}_{name}", shape, F32))
        sem = lambda name: nc.alloc_semaphore(f"{tag}_{name}")
        pairs = shared["bank_pairs"]
        x = [sb(f"x{p}", [P, N]) for p in range(2)]
        xc = [sb(f"xc{p}", [P, N]) for p in range(2)]
        xt = [sb(f"xt{p}", [P, 2, 512]) for p in range(2)]
        total = sb("total", [P, images])
        minus = [sb(f"minus{p}", [P, 1]) for p in range(2)]
        apart = sb("apart", [P, P])
        apart_t = sb("apart_t", [P, P])
        turned = [[pairs[p][:, h, :] for h in range(2)] for p in range(2)]
        gram = [pairs[2][:, p, :] for p in range(2)]
        loaded, summed, minus_ready, centred = [sem(f"loaded{p}") for p in range(2)], sem("summed"), sem("minus_ready"), sem("centred")
        turned_ready, copied, gram_ready, added = sem("turned_ready"), sem("copied"), sem("gram_ready"), sem("added")
        end_step, end_turned, end_copied, end_gram = sem("end_step"), sem("end_turned"), sem("end_copied"), sem("end_gram")
        block = ctx.enter_context(nc.Block())
        ident = shared["ident"]
        stages = [("load", 0), ("centre", 0), ("turn", 1), ("gram", 2)]

        @block.sync
        def _(sp):
            def do(name, b):
                if name == "load":
                    row = sp.snap(b.plus(0).k * 2 + b.p) if not isinstance(b.k, int) else 2 * b.k + b.p
                    if before(b, 2):
                        sp.wait_ge(centred, b.times(1, -1))
                    sp.dma_start(x[b.parity][:, :], x_in[row]).then_inc(loaded[b.parity], 16)
            pipeline(sp, stages, do, images)

        @block.vector
        def _(dve):
            def do(name, b):
                if name == "centre":
                    dve.wait_ge(loaded[b.parity], b.pairs(16))
                    if before(b, 2):
                        dve.wait_ge(centred, b.times(1, -1))
                    nc.vector.tensor_reduce(minus[b.parity][:, :], x[b.parity][:, :], AX.X, ALU.add).then_inc(summed, 1)
                    dve.wait_ge(summed, b.times(1, 1))
                    nc.vector.tensor_scalar(minus[b.parity][:, :], minus[b.parity][:, :], -1.0 / N, None, ALU.mult).then_inc(minus_ready, 1)
                if name == "gram":
                    dve.wait_ge(gram_ready, b.times(1, 1))
                    if before(b, 1):
                        dve.wait_ge(added, b.times(1))
                        nc.vector.tensor_tensor(cov, gram[b.parity][:, 0:P], cov, ALU.add).then_inc(added, 1)
                    else:
                        nc.vector.tensor_copy(cov, gram[b.parity][:, 0:P]).then_inc(added, 1)
            pipeline(dve, stages, do, images)
            dve.wait_ge(end_copied, images)
            nc.vector.memset(apart[:, :], 0.0).then_inc(end_step, 1)
            nc.vector.tensor_reduce(mean, total[:, :], AX.X, ALU.add).then_inc(end_step, 1)
            dve.wait_ge(end_step, 2)
            nc.vector.tensor_scalar(mean, mean, -1.0 / images, None, ALU.mult).then_inc(end_step, 1)
            dve.wait_ge(end_step, 3)
            nc.vector.tensor_scalar(apart[:, 0:images], total[:, :], mean, None, ALU.add).then_inc(end_step, 1)
            dve.wait_ge(end_turned, 1)
            nc.vector.tensor_copy(apart_t[:, :], turned[0][0][:, 0:P]).then_inc(end_step, 1)
            dve.wait_ge(end_gram, 1)
            dve.wait_ge(added, images)
            nc.vector.tensor_scalar(cov, cov, 1.0 / N, None, ALU.mult).then_inc(end_step, 1)
            dve.wait_ge(end_step, 6)
            nc.vector.tensor_tensor(cov, gram[0][:, 0:P], cov, ALU.add).then_inc(end_step, 1)
            dve.wait_ge(end_step, 7)
            nc.vector.tensor_scalar(cov, cov, 1.0 / images, None, ALU.mult).then_inc(end_step, 1)

        @block.gpsimd
        def _(pool):
            def do(name, b):
                if name == "centre":
                    pool.wait_ge(minus_ready, b.times(1, 1))
                    if isinstance(b.k, int):
                        at = 2 * b.k + b.p
                        dst = total[:, at:at + 1]
                    else:
                        dst = total[:, bass.ds(b.k * 2 + b.p, 1)]
                    nc.gpsimd.tensor_tensor(dst, minus[b.parity][:, :], shared["zero"], ALU.subtract).then_inc(end_copied, 1)
            pipeline(pool, stages, do, images)

        @block.scalar
        def _(act):
            def do(name, b):
                if name == "centre":
                    act.wait_ge(minus_ready, b.times(1, 1))
                    if before(b, 2):
                        act.wait_ge(turned_ready, b.times(2, -2))
                    act.wait_ge(end_copied, b.times(1, 1))
                    nc.scalar.activation(xc[b.parity][:, :], x[b.parity][:, :], ACT.Identity, bias=minus[b.parity][:, :]).then_inc(centred, 1)
                if name == "turn":
                    for half in range(2):
                        act.wait_ge(turned_ready, b.times(2, half + 1))
                        if before(b, 2):
                            act.wait_ge(gram_ready, b.times(1, -1))
                        nc.scalar.activation(xt[b.parity][:, half, :], turned[b.parity][half][:, :], ACT.Copy).then_inc(copied, 1)
            pipeline(act, stages, do, images)

        @block.tensor
        def _(pe):
            def do(name, b):
                if name == "turn":
                    pe.wait_ge(centred, b.times(1, 1))
                    for half in range(2):
                        if before(b, 2):
                            pe.wait_ge(copied, b.times(2, half - 3))
                        for c in range(4):
                            at = 512 * half + P * c
                            mm = nc.tensor.transpose(turned[b.parity][half][:, P * c:P * c + P], xc[b.parity][:, at:at + P], ident)
                        mm.then_inc(turned_ready, 1)
                if name == "gram":
                    pe.wait_ge(copied, b.times(2, 2))
                    if before(b, 2):
                        pe.wait_ge(added, b.times(1, -1))
                    for c in range(KC):
                        block_t = xt[b.parity][:, c // 4, P * (c % 4):P * (c % 4) + P]
                        mm = nc.tensor.matmul(gram[b.parity][:, 0:P], block_t, block_t, start=(c == 0), stop=(c == KC - 1))
                    mm.then_inc(gram_ready, 1)
            pipeline(pe, stages, do, images)
            pe.wait_ge(end_step, 4)
            pe.wait_ge(copied, 2 * images)
            nc.tensor.transpose(turned[0][0][:, 0:P], apart[:, :], ident).then_inc(end_turned, 1)
            pe.wait_ge(end_step, 5)
            pe.wait_ge(added, images)
            nc.tensor.matmul(gram[0][:, 0:P], apart_t[:, :], apart_t[:, :], start=True, stop=True).then_inc(end_gram, 1)


def whiten(nc, M, shared, mean, cov, move, offset):
    with ExitStack() as ctx:
        sb = lambda name, shape: ctx.enter_context(nc.sbuf_tensor(f"w_{name}", shape, F32))
        sem = lambda name: nc.alloc_semaphore(f"w_{name}")
        a = sb("a", [P, 2, P])
        own = sb("own", [P, P])
        diagonal = sb("diagonal", [P, 2])
        trace = sb("trace", [P, 2])
        inverse = sb("inverse", [P, 2])
        ratio = sb("ratio", [P, 1])
        root = sb("root", [P, 1])
        power = sb("power", [P, 1])
        three = sb("three", [P, P])
        ridge = sb("ridge", [P, P])
        yz = sb("yz", [P, 2, 2, P])
        t = sb("t", [P, 2, P])
        p_trace, p_t, p_yz, p_end = [shared["bank_pairs"][i // 2][:, i % 2, :] for i in range(4)]
        setup, diagonal_ready, trace_ready, first_ready = sem("setup"), sem("diagonal_ready"), sem("trace_ready"), sem("first_ready")
        zy_made, t_ready, yz_made, yz_ready = sem("zy_made"), sem("t_ready"), sem("yz_made"), sem("yz_ready")
        ratio_ready, root_ready, product, moved, offset_made = (
            sem("ratio_ready"), sem("root_ready"), sem("product"), sem("moved"), sem("offset_made"))
        block = ctx.enter_context(nc.Block())

        @block.vector
        def _(dve):
            nc.vector.memset(power[:, :], 0.5).then_inc(ratio_ready, 1)
            nc.vector.tensor_scalar(three[:, :], M["ident"], 0.75, None, ALU.mult).then_inc(setup, 1)
            nc.vector.tensor_scalar(ridge[:, :], M["ident"], EPS_COV, None, ALU.mult).then_inc(setup, 1)
            for s in range(2):
                nc.vector.tensor_tensor(a[:, s, :], cov[s], M["block"], ALU.mult).then_inc(setup, 1)
            dve.wait_ge(setup, 4)
            for s in range(2):
                nc.vector.tensor_tensor(a[:, s, :], a[:, s, :], ridge[:, :], ALU.add).then_inc(setup, 1)
            dve.wait_ge(setup, 6)
            for s in range(2):
                nc.vector.tensor_tensor(own[:, :], a[:, s, :], M["ident"], ALU.mult).then_inc(setup, 1)
                dve.wait_ge(setup, 7 + 2 * s)
                nc.vector.tensor_reduce(diagonal[:, s:s + 1], own[:, :], AX.X, ALU.add).then_inc(setup, 1)
                dve.wait_ge(setup, 8 + 2 * s)
            nc.vector.tensor_copy(yz[:, 0, 1, :], M["ident"]).then_inc(diagonal_ready, 1)
            nc.vector.tensor_copy(yz[:, 1, 1, :], M["ident"]).then_inc(diagonal_ready, 1)
            dve.wait_ge(trace_ready, 1)
            nc.vector.tensor_copy(trace[:, :], p_trace[:, 0:2]).then_inc(setup, 1)
            dve.wait_ge(setup, 11)
            nc.vector.reciprocal(inverse[:, :], trace[:, :]).then_inc(setup, 1)
            dve.wait_ge(setup, 12)
            for s in range(2):
                nc.vector.tensor_scalar(yz[:, s, 0, :], a[:, s, :], inverse[:, s:s + 1], None, ALU.mult).then_inc(yz_ready if s else first_ready, 1)
            nc.vector.tensor_tensor(ratio[:, :], trace[:, 1:2], inverse[:, 0:1], ALU.mult).then_inc(ratio_ready, 1)
            with dve.Fori(0, ROOT_STEPS) as k:
                dve.wait_ge(zy_made, k + 1)
                for s in range(2):
                    nc.vector.scalar_tensor_tensor(out=t[:, s, :], in0=p_t[:, P * s:P * s + P], scalar=-0.25, in1=three[:, :],
                                                   op0=ALU.mult, op1=ALU.add).then_inc(t_ready, 1)
                dve.wait_ge(yz_made, k + 1)
                nc.vector.tensor_copy(yz[:, :, :, :].rearrange("p s y c -> p (s y c)"), p_yz[:, :]).then_inc(yz_ready, 1)
            dve.wait_ge(product, 1)
            dve.wait_ge(root_ready, 1)
            nc.vector.tensor_scalar(move, p_end[:, 0:P], root[:, :], None, ALU.mult).then_inc(moved, 1)
            dve.wait_ge(offset_made, 1)
            nc.vector.tensor_tensor(offset, mean[1], p_trace[:, 0:1], ALU.subtract).then_inc(moved, 1)

        @block.gpsimd
        def _(pool):
            pool.wait_ge(ratio_ready, 2)
            nc.gpsimd.tensor_tensor(root[:, :], ratio[:, :], power[:, :], ALU.pow).then_inc(root_ready, 1)

        @block.tensor
        def _(pe):
            pe.wait_ge(diagonal_ready, 2)
            nc.tensor.matmul(p_trace[:, 0:2], M["block"], diagonal[:, :], start=True, stop=True).then_inc(trace_ready, 1)
            pe.wait_ge(first_ready, 1)
            with pe.Fori(0, ROOT_STEPS) as k:
                pe.wait_ge(yz_ready, k + 1)
                for s in range(2):
                    mm = nc.tensor.matmul(p_t[:, P * s:P * s + P], yz[:, s, 1, :], yz[:, s, 0, :], start=True, stop=True)
                mm.then_inc(zy_made, 1)
                pe.wait_ge(t_ready, k * 2 + 2)
                for s in range(2):
                    for part in range(2):
                        dst, m = p_yz[:, P * (2 * s + part):P * (2 * s + part) + P], yz[:, s, part, :]
                        nc.tensor.matmul(dst, m, t[:, s, :], start=True, stop=False)
                        mm = nc.tensor.matmul(dst, t[:, s, :], m, start=False, stop=True)
                mm.then_inc(yz_made, 1)
            pe.wait_ge(yz_ready, ROOT_STEPS + 1)
            nc.tensor.matmul(p_end[:, 0:P], yz[:, 0, 1, :], yz[:, 1, 0, :], start=True, stop=True).then_inc(product, 1)
            pe.wait_ge(moved, 1)
            nc.tensor.matmul(p_trace[:, 0:1], move, mean[0], start=True, stop=True).then_inc(offset_made, 1)


class GroupNorm:

    def __init__(self, sb, name, gain, shift):
        self.parts = [sb(f"{name}_parts{p}", [P, 12]) for p in range(2)]
        self.pair = [sb(f"{name}_pair{p}", [P, 2]) for p in range(2)]
        self.group = [sb(f"{name}_group{p}", [P, 2]) for p in range(2)]
        self.var = [sb(f"{name}_var{p}", [P, 1]) for p in range(2)]
        self.rstd = [sb(f"{name}_rstd{p}", [P, 1]) for p in range(2)]
        self.a = [sb(f"{name}_a{p}", [P, 1]) for p in range(2)]
        self.b = [sb(f"{name}_b{p}", [P, 1]) for p in range(2)]
        self.gain, self.shift = gain, shift


GN_STEPS = 10


def norm_statistics(nc, dve, g, p, x, b, step, begun):
    at = lambda n: b.times(GN_STEPS, n)
    nc.vector.bn_stats(g.parts[p][:, 0:6], x[:, 0:512]).then_inc(step, 1)
    nc.vector.bn_stats(g.parts[p][:, 6:12], x[:, 512:N]).then_inc(step, 1)
    dve.wait_ge(step, at(2))
    dve.sem_inc(begun, 1)
    nc.vector.bn_aggr(g.pair[p][:, :], g.parts[p][:, :]).then_inc(step, 1)
    dve.wait_ge(step, at(3))
    nc.vector.scalar_tensor_tensor(out=g.pair[p][:, 1:2], in0=g.pair[p][:, 0:1], scalar=g.pair[p][:, 0:1],
                                   in1=g.pair[p][:, 1:2], op0=ALU.mult, op1=ALU.add).then_inc(step, 1)


def norm_variance(nc, dve, g, p, ps, b, step):
    at = lambda n: b.times(GN_STEPS, n)
    nc.vector.tensor_copy(g.group[p][:, :], ps).then_inc(step, 1)
    dve.wait_ge(step, at(5))
    nc.vector.scalar_tensor_tensor(out=g.var[p][:, :], in0=g.group[p][:, 0:1], scalar=g.group[p][:, 0:1],
                                   in1=g.group[p][:, 1:2], op0=ALU.mult, op1=ALU.subtract).then_inc(step, 1)
    dve.wait_ge(step, at(6))
    nc.vector.tensor_scalar(g.var[p][:, :], g.var[p][:, :], -1.0, EPS_GN, ALU.mult, ALU.add).then_inc(step, 1)


def norm_factors(nc, dve, g, p, b, step):
    at = lambda n: b.times(GN_STEPS, n)
    nc.vector.tensor_tensor(g.a[p][:, :], g.rstd[p][:, :], g.gain, ALU.mult).then_inc(step, 1)
    dve.wait_ge(step, at(8))
    nc.vector.scalar_tensor_tensor(out=g.b[p][:, :], in0=g.group[p][:, 0:1], scalar=g.a[p][:, :], in1=g.shift,
                                   op0=ALU.mult, op1=ALU.subtract).then_inc(step, 1)
    dve.wait_ge(step, at(9))
    nc.vector.tensor_scalar(g.b[p][:, :], g.b[p][:, :], -1.0, None, ALU.mult).then_inc(step, 1)


def gate(nc, M, V, shared, halves, move, offset, x_in, pos_in, h_out, normed_out, gated_out):
    with ExitStack() as ctx:
        sb = lambda name, shape: ctx.enter_context(nc.sbuf_tensor(f"g_{name}", shape, F32))
        sem = lambda name: nc.alloc_semaphore(f"g_{name}")
        pair = lambda name, shape: [sb(f"{name}{p}", shape) for p in range(2)]
        flat = lambda t: t[:, :, :].rearrange("p a b -> p (a b)")
        x0, h, xg, xs = pair("x0", [P, N]), pair("h", [P, N]), pair("xg", [P, N]), pair("xs", [P, N])
        pos = sb("pos", [P, N])
        th1, u1 = sb("th1", [96, N]), sb("u1", [96, N])
        field = sb("field", [96, SIDE + 2, SIDE])
        th2, u2, s2 = sb("th2", [64, 512]), sb("u2", [64, 512]), sb("s2", [64, 512])
        th3, gated, normed = sb("th3", [P, N]), sb("gated", [P, N]), sb("normed", [P, N])
        power = sb("power", [P, 1])
        g1, g2 = GroupNorm(sb, "g1", V["c_pre_g"], V["c_pre_b"]), GroupNorm(sb, "g2", V["c_norm_g"], V["c_norm_b"])
        p_h, p_s1, p_s3, small = shared["bank_pairs"]
        p_s2, p_g = small[:, 0:1, :], small[:, 1:2, :]
        const_ready, pos_loaded, loaded, h_made, h_ready, h_stored = (
            sem("const_ready"), sem("pos_loaded"), [sem(f"loaded{p}") for p in range(2)], sem("h_made"), sem("h_ready"),
            [sem(f"h_stored{p}") for p in range(2)])
        step1, step2, group1, group2, rstd1, rstd2 = (
            sem("step1"), sem("step2"), sem("group1"), sem("group2"), sem("rstd1"), sem("rstd2"))
        xg_ready, x_ready = sem("xg_ready"), sem("x_ready")
        s1_made, th1_ready, u1_ready, field_ready = sem("s1_made"), sem("th1_ready"), sem("u1_ready"), sem("field_ready")
        s2_made, th2_ready, u2_ready, s2_ready = sem("s2_made"), sem("th2_ready"), sem("u2_ready"), sem("s2_ready")
        s3_made, th3_ready, gated_ready, normed_ready = sem("s3_made"), sem("th3_ready"), sem("gated_ready"), sem("normed_ready")
        gated_stored, normed_stored = sem("gated_stored"), sem("normed_stored")
        block = ctx.enter_context(nc.Block())
        stages = [("load", 0), ("move", 1), ("gate2", 3), ("conv1", 2), ("conv3", 3), ("stats1", 1), ("field", 2), ("group1", 1),
                  ("conv2", 2), ("factors1", 1), ("gate3", 3), ("out", 3), ("norm1", 1), ("stats2", 2), ("group2", 2), ("factors2", 2)]

        @block.sync
        def _(sp):
            sp.dma_start(pos[:, :], pos_in).then_inc(pos_loaded, 16)

            def do(name, b):
                p = b.parity
                if name not in ("load", "stats1", "out"):
                    return
                row = 2 * b.k + b.p if isinstance(b.k, int) else sp.snap(b.k * 2 + b.p)
                if name == "load":
                    if before(b, 2):
                        sp.wait_ge(h_made, b.times(1, -1))
                    sp.dma_start(x0[p][:, :], x_in[row]).then_inc(loaded[p], 16)
                if name == "stats1":
                    sp.wait_ge(h_ready, b.times(1, 1))
                    sp.dma_start(h_out[row], h[p][:, :]).then_inc(h_stored[p], 16)
                if name == "out":
                    sp.wait_ge(gated_ready, b.times(1, 1))
                    sp.dma_start(gated_out[row], gated[:, :]).then_inc(gated_stored, 16)
                    sp.wait_ge(normed_ready, b.times(1, 1))
                    sp.dma_start(normed_out[row], normed[:, :]).then_inc(normed_stored, 16)
            pipeline(sp, stages, do)
            for stored, n in ((h_stored[0], NB // 2), (h_stored[1], NB // 2), (gated_stored, NB), (normed_stored, NB)):
                sp.wait_ge(stored, 16 * n)

        @block.gpsimd
        def _(pool):
            def do(name, b):
                p = b.parity
                if name in ("factors1", "factors2"):
                    g, step, rstd = (g1, step1, rstd1) if name == "factors1" else (g2, step2, rstd2)
                    pool.wait_ge(step, b.times(GN_STEPS, 7))
                    nc.gpsimd.tensor_tensor(g.rstd[p][:, :], g.var[p][:, :], power[:, :], ALU.pow).then_inc(rstd, 1)
                if name == "norm1":
                    pool.wait_ge(xg_ready, b.times(1, 1))
                    if before(b, 2):
                        pool.wait_ge(gated_ready, b.times(1, -1))
                        pool.wait_ge(normed_ready, b.times(1, -1))
                    nc.gpsimd.tensor_tensor(xs[p][:, :], xg[p][:, :], pos[:, :], ALU.add).then_inc(x_ready, 1)
            pool.wait_ge(pos_loaded, 16)
            pool.wait_ge(const_ready, 2)
            pipeline(pool, stages, do)

        @block.tensor
        def _(pe):
            half_of = lambda t, half: t[:, 512 * half:512 * half + 512]

            def do(name, b):
                p = b.parity
                if name == "move":
                    pe.wait_ge(loaded[p], b.pairs(16))
                    if before(b, 1):
                        pe.wait_ge(h_ready, b.times(1))
                    for half in range(2):
                        mm = nc.tensor.matmul(p_h[:, half, :], move, half_of(x0[p], half), start=True, stop=True)
                    mm.then_inc(h_made, 1)
                if name == "group1":
                    pe.wait_ge(step1, b.times(GN_STEPS, 4))
                    nc.tensor.matmul(p_g[:, 0, 0:2], M["mean4"], g1.pair[p][:, :], start=True, stop=True).then_inc(group1, 1)
                if name == "group2":
                    pe.wait_ge(step2, b.times(GN_STEPS, 4))
                    if before(b, 1):
                        pe.wait_ge(th3_ready, b.times(1))
                    nc.tensor.matmul(p_s3[:, 0, 0:2], M["mean4"], g2.pair[p][:, :], start=True, stop=True).then_inc(group2, 1)
                if name == "conv1":
                    pe.wait_ge(x_ready, b.times(1, 1))
                    if before(b, 1):
                        pe.wait_ge(th1_ready, b.times(1))
                        pe.wait_ge(u1_ready, b.times(1))
                    for half in range(2):
                        mm = nc.tensor.matmul(p_s1[0:96, half, :], M["c_s1"], half_of(xs[p], half), start=True, stop=True)
                    mm.then_inc(s1_made, 1)
                if name == "conv2":
                    pe.wait_ge(field_ready, b.times(3, 3))
                    if before(b, 1):
                        pe.wait_ge(th2_ready, b.times(1))
                        pe.wait_ge(u2_ready, b.times(1))
                    for half in range(2):
                        for dy in range(3):
                            at = SIDE // 2 * half + dy
                            rows = field[:, at:at + SIDE // 2, :].rearrange("p a b -> p (a b)")
                            mm = nc.tensor.matmul(p_s2[32 * half:32 * half + 32, 0, :], M[f"c_s2{dy}"], rows,
                                                  start=(dy == 0), stop=(dy == 2), tile_position=(0, 32 * half),
                                                  skip_group_check=True)
                    mm.then_inc(s2_made, 1)
                if name == "conv3":
                    pe.wait_ge(s2_ready, b.times(1, 1))
                    pe.wait_ge(step2, b.times(GN_STEPS, 5))
                    for half in range(2):
                        rows = slice(32 * half, 32 * half + 32)
                        mm = nc.tensor.matmul(p_s3[:, half, :], M["c_s3"][rows, :], s2[rows, :], start=True, stop=True)
                    mm.then_inc(s3_made, 1)
            pipeline(pe, stages, do)

        @block.scalar
        def _(act):
            def do(name, b):
                p = b.parity
                if name == "move":
                    act.wait_ge(h_made, b.times(1, 1))
                    if before(b, 2):
                        act.wait_ge(h_stored[p], b.plus(-2).pairs(16))
                    nc.scalar.activation(h[p][:, :], flat(p_h), ACT.Identity, bias=offset).then_inc(h_ready, 1)
                if name == "conv1":
                    act.wait_ge(s1_made, b.times(1, 1))
                    if before(b, 1):
                        act.wait_ge(field_ready, b.times(3))
                    nc.scalar.activation(th1[:, :], flat(p_s1)[0:96, :], ACT.Tanh, bias=halves[0], scale=0.5).then_inc(th1_ready, 1)
                if name == "gate2":
                    act.wait_ge(s2_made, b.times(1, 1))
                    if before(b, 1):
                        act.wait_ge(s2_ready, b.times(1))
                    nc.scalar.activation(th2[:, :], p_s2[0:64, 0, :], ACT.Tanh, bias=halves[1], scale=0.5).then_inc(th2_ready, 1)
                if name == "norm1":
                    act.wait_ge(step1, b.times(GN_STEPS, GN_STEPS))
                    if before(b, 2):
                        act.wait_ge(x_ready, b.times(1, -1))
                    nc.scalar.activation(xg[p][:, :], h[p][:, :], ACT.Identity, bias=g1.b[p][:, :], scale=g1.a[p][:, :]).then_inc(xg_ready, 1)
                if name == "gate3":
                    act.wait_ge(s3_made, b.times(1, 1))
                    if before(b, 1):
                        act.wait_ge(gated_ready, b.times(1))
                    nc.scalar.activation(th3[:, :], flat(p_s3), ACT.Tanh, bias=halves[2], scale=0.5).then_inc(th3_ready, 1)
                if name == "out":
                    act.wait_ge(step2, b.times(GN_STEPS, GN_STEPS))
                    if before(b, 1):
                        act.wait_ge(normed_stored, b.times(16))
                    nc.scalar.activation(normed[:, :], xs[p][:, :], ACT.Identity, bias=g2.b[p][:, :], scale=g2.a[p][:, :]).then_inc(normed_ready, 1)
            pipeline(act, stages, do)

        @block.vector
        def _(dve):
            nc.vector.memset(power[:, :], -0.5).then_inc(const_ready, 1)
            nc.vector.memset(field[:, :, :], 0.0).then_inc(const_ready, 1)
            dve.wait_ge(const_ready, 2)

            def do(name, b):
                p = b.parity
                if name == "stats1":
                    dve.wait_ge(h_ready, b.times(1, 1))
                    norm_statistics(nc, dve, g1, p, h[p], b, step1, const_ready)
                if name == "stats2":
                    norm_statistics(nc, dve, g2, p, xs[p], b, step2, const_ready)
                if name in ("factors1", "factors2"):
                    g, step, group, rstd, sums = (g1, step1, group1, rstd1, p_g) if name == "factors1" else (g2, step2, group2, rstd2, p_s3)
                    dve.wait_ge(group, b.times(1, 1))
                    norm_variance(nc, dve, g, p, sums[:, 0, 0:2], b, step)
                    dve.wait_ge(rstd, b.times(1, 1))
                    norm_factors(nc, dve, g, p, b, step)
                if name == "conv1":
                    dve.wait_ge(th1_ready, b.times(1, 1))
                    if before(b, 1):
                        dve.wait_ge(field_ready, b.times(3))
                    nc.vector.tensor_scalar(u1[:, :], flat(p_s1)[0:96, :], V["c_s1b"], 0.5, ALU.add, ALU.mult).then_inc(u1_ready, 1)
                if name == "field":
                    dve.wait_ge(u1_ready, b.times(1, 1))
                    if before(b, 1):
                        dve.wait_ge(s2_made, b.times(1))
                    for dx in range(3):
                        rows = slice(32 * dx, 32 * dx + 32)
                        dst, src = slice(max(0, 1 - dx), min(SIDE, SIDE + 1 - dx)), slice(max(0, dx - 1), min(SIDE, SIDE - 1 + dx))
                        a = th1[rows, :].rearrange("p (y x) -> p y x", x=SIDE)[:, :, src]
                        c = u1[rows, :].rearrange("p (y x) -> p y x", x=SIDE)[:, :, src]
                        nc.vector.scalar_tensor_tensor(out=field[rows, 1:SIDE + 1, dst], in0=a, scalar=1.0, in1=c,
                                                       op0=ALU.add, op1=ALU.mult).then_inc(field_ready, 1)
                if name == "gate2":
                    dve.wait_ge(th2_ready, b.times(1, 1))
                    nc.vector.tensor_scalar(u2[:, :], p_s2[0:64, 0, :], halves[3], 0.5, ALU.add, ALU.mult).then_inc(u2_ready, 1)
                    dve.wait_ge(u2_ready, b.times(1, 1))
                    if before(b, 1):
                        dve.wait_ge(s3_made, b.times(1))
                    nc.vector.scalar_tensor_tensor(out=s2[:, :], in0=th2[:, :], scalar=1.0, in1=u2[:, :],
                                                   op0=ALU.add, op1=ALU.mult).then_inc(s2_ready, 1)
                if name == "gate3":
                    dve.wait_ge(th3_ready, b.times(1, 1))
                    if before(b, 1):
                        dve.wait_ge(gated_stored, b.times(16))
                    nc.vector.scalar_tensor_tensor(out=gated[:, :], in0=th3[:, :], scalar=1.0, in1=xs[p][:, :],
                                                   op0=ALU.add, op1=ALU.mult).then_inc(gated_ready, 1)
            pipeline(dve, stages, do)


def feed_forward(nc, M, V, shared, half_b1, ff_in, h_in, out):
    with ExitStack() as ctx:
        sb = lambda name, shape: ctx.enter_context(nc.sbuf_tensor(f"f_{name}", shape, F32))
        sem = lambda name: nc.alloc_semaphore(f"f_{name}")
        pair = lambda name, shape: [sb(f"{name}{p}", shape) for p in range(2)]
        flat = lambda t: t[:, :, :].rearrange("p a b -> p (a b)")
        ff, h, th, u, s = pair("ff", [P, N]), pair("h", [P, N]), pair("th", [P, N]), pair("u", [P, N]), pair("s", [P, N])
        f2, fin, hb, z = pair("f2", [P, N]), pair("fin", [P, N]), pair("hb", [P, N]), pair("z", [P, N])
        power = sb("power", [P, 1])
        g = GroupNorm(sb, "g", V["c_post_g"], V["c_post_b"])
        p_2, p_3, p_g, _ = shared["bank_pairs"]
        const_ready, ff_loaded, h_loaded = sem("const_ready"), [sem(f"ff_loaded{p}") for p in range(2)], [sem(f"h_loaded{p}") for p in range(2)]
        th_ready, u_ready, s_ready, f2_made, f2_ready, f3_made, fin_ready = (
            sem("th_ready"), sem("u_ready"), sem("s_ready"), sem("f2_made"), sem("f2_ready"), sem("f3_made"), sem("fin_ready"))
        step, group, rstd, hb_ready, z_ready, stored = (
            sem("step"), sem("group"), sem("rstd"), sem("hb_ready"), sem("z_ready"), [sem(f"stored{p}") for p in range(2)])
        block = ctx.enter_context(nc.Block())
        stages = [("load", 0), ("final", 3), ("silu", 1), ("w2", 1), ("stats", 2), ("factors", 2), ("w3", 1)]

        @block.sync
        def _(sp):
            def do(name, b):
                p = b.parity
                if name not in ("load", "silu", "final"):
                    return
                row = 2 * b.k + b.p if isinstance(b.k, int) else sp.snap(b.k * 2 + b.p)
                if name == "load":
                    if before(b, 2):
                        sp.wait_ge(u_ready, b.times(1, -1))
                        sp.wait_ge(th_ready, b.times(1, -1))
                    sp.dma_start(ff[p][:, :], ff_in[row]).then_inc(ff_loaded[p], 16)
                if name == "silu":
                    if before(b, 2):
                        sp.wait_ge(hb_ready, b.times(1, -1))
                    sp.dma_start(h[p][:, :], h_in[row]).then_inc(h_loaded[p], 16)
                if name == "final":
                    sp.wait_ge(z_ready, b.times(1, 1))
                    sp.dma_start(out[row], z[p][:, :]).then_inc(stored[p], 16)
            pipeline(sp, stages, do)
            for p in range(2):
                sp.wait_ge(stored[p], 16 * NB // 2)

        @block.gpsimd
        def _(pool):
            def do(name, b):
                p = b.parity
                if name == "factors":
                    pool.wait_ge(step, b.times(GN_STEPS, 7))
                    nc.gpsimd.tensor_tensor(g.rstd[p][:, :], g.var[p][:, :], power[:, :], ALU.pow).then_inc(rstd, 1)
            pool.wait_ge(const_ready, 1)
            pipeline(pool, stages, do)

        @block.tensor
        def _(pe):
            half_of = lambda t, half: t[:, 512 * half:512 * half + 512]

            def do(name, b):
                p = b.parity
                if name == "w2":
                    pe.wait_ge(s_ready, b.times(1, 1))
                    if before(b, 1):
                        pe.wait_ge(f2_ready, b.times(1))
                    for half in range(2):
                        mm = nc.tensor.matmul(p_2[:, half, :], M["c_w2"], half_of(s[p], half), start=True, stop=True)
                    mm.then_inc(f2_made, 1)
                if name == "w3":
                    pe.wait_ge(f2_ready, b.times(1, 1))
                    if before(b, 1):
                        pe.wait_ge(fin_ready, b.times(1))
                    for half in range(2):
                        mm = nc.tensor.matmul(p_3[:, half, :], M["c_out"], half_of(f2[p], half), start=True, stop=True)
                    mm.then_inc(f3_made, 1)
                if name == "stats":
                    pe.wait_ge(step, b.times(GN_STEPS, 4))
                    if before(b, 1):
                        pe.wait_ge(step, b.times(GN_STEPS, 5 - GN_STEPS))
                    nc.tensor.matmul(p_g[:, 0, 0:2], M["mean4"], g.pair[p][:, :], start=True, stop=True).then_inc(group, 1)
            pipeline(pe, stages, do)

        @block.scalar
        def _(act):
            def do(name, b):
                p = b.parity
                if name == "silu":
                    act.wait_ge(ff_loaded[p], b.pairs(16))
                    if before(b, 2):
                        act.wait_ge(s_ready, b.times(1, -1))
                    nc.scalar.activation(th[p][:, :], ff[p][:, :], ACT.Tanh, bias=half_b1, scale=0.5).then_inc(th_ready, 1)
                if name == "w2":
                    act.wait_ge(f2_made, b.times(1, 1))
                    if before(b, 2):
                        act.wait_ge(f3_made, b.times(1, -1))
                    nc.scalar.activation(f2[p][:, :], flat(p_2), ACT.Identity, bias=V["c_ff_b2"]).then_inc(f2_ready, 1)
                if name == "w3":
                    act.wait_ge(f3_made, b.times(1, 1))
                    if before(b, 2):
                        act.wait_ge(z_ready, b.times(1, -1))
                    nc.scalar.activation(fin[p][:, :], flat(p_3), ACT.Identity, bias=V["c_out_b"]).then_inc(fin_ready, 1)
                if name == "factors":
                    act.wait_ge(step, b.times(GN_STEPS, GN_STEPS))
                    act.wait_ge(h_loaded[p], b.pairs(16))
                    if before(b, 2):
                        act.wait_ge(z_ready, b.times(1, -1))
                    nc.scalar.activation(hb[p][:, :], h[p][:, :], ACT.Identity, bias=g.b[p][:, :]).then_inc(hb_ready, 1)
            pipeline(act, stages, do)

        @block.vector
        def _(dve):
            nc.vector.memset(power[:, :], -0.5).then_inc(const_ready, 1)

            def do(name, b):
                p = b.parity
                if name == "silu":
                    dve.wait_ge(ff_loaded[p], b.pairs(16))
                    if before(b, 2):
                        dve.wait_ge(s_ready, b.times(1, -1))
                    nc.vector.tensor_scalar(u[p][:, :], ff[p][:, :], V["c_ff_b1"], 0.5, ALU.add, ALU.mult).then_inc(u_ready, 1)
                    dve.wait_ge(u_ready, b.times(1, 1))
                    dve.wait_ge(th_ready, b.times(1, 1))
                    if before(b, 2):
                        dve.wait_ge(f2_made, b.times(1, -1))
                    nc.vector.scalar_tensor_tensor(out=s[p][:, :], in0=th[p][:, :], scalar=1.0, in1=u[p][:, :],
                                                   op0=ALU.add, op1=ALU.mult).then_inc(s_ready, 1)
                if name == "stats":
                    dve.wait_ge(fin_ready, b.times(1, 1))
                    norm_statistics(nc, dve, g, p, fin[p], b, step, const_ready)
                if name == "factors":
                    dve.wait_ge(group, b.times(1, 1))
                    norm_variance(nc, dve, g, p, p_g[:, 0, 0:2], b, step)
                    dve.wait_ge(rstd, b.times(1, 1))
                    norm_factors(nc, dve, g, p, b, step)
                if name == "final":
                    dve.wait_ge(hb_ready, b.times(1, 1))
                    if before(b, 2):
                        dve.wait_ge(stored[p], b.plus(-2).pairs(16))
                    nc.vector.scalar_tensor_tensor(out=z[p][:, :], in0=fin[p][:, :], scalar=g.a[p][:, :], in1=hb[p][:, :],
                                                   op0=ALU.mult, op1=ALU.add).then_inc(z_ready, 1)
            pipeline(dve, stages, do)


def padded_heads(w):
    t = np.zeros((2, 4, 32, w.shape[0]), w.dtype)
    t[:, :, :HD] = w.T.reshape(2, 4, HD, w.shape[0])
    return t.reshape(2, P, w.shape[0])


def matrices(i):
    m = {}
    q, k, v = np.split(i["L0_conv_qkv_w"], 3)
    m["a_q"], m["a_k"], m["a_v"] = q.T, k.T, v.T
    m["a_proj0"], m["a_proj1"] = padded_heads(i["L0_conv_proj_w"])
    for n in "qkv":
        m["c_" + n] = i["L2_conv_w" + n].T
    for h in range(2):
        m[f"c_dq{h}"], m[f"c_dk{h}"] = i[f"L2_conv_wq{h}"].T, i[f"L2_conv_wk{h}"].T
    m["c_vd"] = np.concatenate([i["L2_conv_wv0"].T, i["L2_conv_wv1"].T], 1)
    m["c_ff0"], m["c_ff1"] = padded_heads(i["L2_conv_ff_w1"][:, :P])
    m["c_ff2"] = i["L2_conv_ff_w1"][:, P:].T
    m["c_w2"], m["c_out"] = i["L2_conv_ff_w2"].T, i["L2_conv_out_w"].T
    w1 = np.zeros((P, 3, 32), np.float32)
    w1[:, :, :16] = i["L2_conv_sa_w1"][:, :, 0, 0].T[:, None, :]
    m["c_s1"] = w1.reshape(P, 96)
    w2 = i["L2_conv_sa_w2"]
    for dy in range(3):
        t = np.zeros((3, 32, 32), np.float32)
        t[:, :16, :16] = w2[:, :, dy, :].transpose(2, 1, 0)
        m[f"c_s2{dy}"] = t.reshape(96, 32)
    s3 = np.zeros((2, 32, P), np.float32)
    s3[:, :16] = i["L2_conv_sa_w3"][0, :, 0, 0][:, None]
    m["c_s3"] = s3.reshape(64, P)
    t = np.zeros((P, 2, 32), np.float32)
    t[:, 0, :HD], t[:, 1, :HD] = i["L3_conv_Wq"].T, i["L3_conv_Wk"].T
    m["d_qk"] = t.reshape(P, 64)
    m["d_v"] = i["L3_conv_Wv"].T
    at = np.arange(P)
    m["ident"] = np.eye(P, dtype=np.float32)
    m["ones"] = np.ones((P, P), np.float32)
    m["pick"] = (at[:, None] == 32 * np.arange(4)[None] + 16).astype(np.float32)
    m["mean4"] = ((at[:, None] // 4) == (at[None] // 4)).astype(np.float32) / 4
    m["block"] = ((at[:, None] // CG) == (at[None] // CG)).astype(np.float32)
    return m


def vectors(i):
    v = {}
    b = i["L0_conv_qkv_b"]
    v["a_qb"], v["a_kb"] = b[:P], b[P:2 * P]
    t = padded_heads(b[None, 2 * P:])
    v["a_vb0"], v["a_vb1"] = t[0, :, 0], t[1, :, 0]
    v["a_pb"] = i["L0_conv_proj_b"]
    for n in ("pre_g", "pre_b", "norm_g", "norm_b", "post_g", "post_b", "ff_b1", "ff_b2", "out_b"):
        v["c_" + n] = i["L2_conv_" + n]
    t = np.zeros((3, 32), np.float32)
    t[:, :16] = i["L2_conv_sa_b1"]
    v["c_s1b"] = t.reshape(96)
    t = np.zeros((2, 32), np.float32)
    t[:, :16] = i["L2_conv_sa_b2"]
    v["c_s2b"] = t.reshape(64)
    v["c_s3b"] = np.repeat(i["L2_conv_sa_b3"], P)
    t = np.zeros((2, 32), np.float32)
    t[0, :HD], t[1, :HD] = i["L3_conv_bq"], i["L3_conv_bk"]
    v["d_qkb"] = t.reshape(64)
    v["d_vb"], v["d_gamma"] = i["L3_conv_bv"], np.repeat(i["L3_conv_gamma"], P)
    return v


def packed(named):
    where, at = {}, 0
    for n, a in named.items():
        a = a if a.ndim == 2 else a[:, None]
        where[n] = (a.shape[0], at, at + a.shape[1])
        at += a.shape[1]
    out = np.zeros((P, at), np.float32)
    for n, a in named.items():
        rows, first, last = where[n]
        out[:rows, first:last] = a if a.ndim == 2 else a[:, None]
    return out, where


def program(nc, x, style, pos, mats, vecs, at, vat, out, scratch):
    with ExitStack() as ctx:
        sb = lambda name, shape: ctx.enter_context(nc.sbuf_tensor(name, shape, F32))
        sem = lambda name: ctx.enter_context(nc.semaphore(name))
        wt, vt = sb("mats_sb", [P, mats.shape[1]]), sb("vecs_sb", [P, vecs.shape[1]])
        made = sb("made", [P, 16])
        zero = made[:, 0:1]
        a_qb, a_out = made[:, 1:2], made[:, 2:3]
        halves = [made[0:96, 3:4], made[0:64, 4:5], made[:, 5:6]]
        half_b1 = made[:, 6:7]
        mean = [made[:, 7:8], made[:, 8:9]]
        offset = made[:, 9:10]
        M = {n: wt[0:rows, a:b] for n, (rows, a, b) in at.items()}
        V = {n: vt[0:rows, a:b] for n, (rows, a, b) in vat.items()}
        bank_pairs = [ctx.enter_context(nc.psum_tensor(f"banks{i}", [P, 2, 512], F32))[:, :, :] for i in range(4)]
        shared = {"bank_pairs": bank_pairs, "zero": zero, "ident": M["ident"], "ones": M["ones"], "pick": M["pick"]}
        head_scale = float(P) ** -0.5

        constants_loaded, product_made, setup_made = sem("constants_loaded"), sem("product_made"), sem("setup_made")
        ps = bank_pairs[0][:, 0, :]
        with nc.Block() as block:
            @block.sync
            def _(sp):
                sp.dma_start(wt[:, :], mats).then_inc(constants_loaded, 16)
                sp.dma_start(vt[:, :], vecs).then_inc(constants_loaded, 16)

            @block.tensor
            def _(pe):
                pe.wait_ge(constants_loaded, 32)
                nc.tensor.matmul(ps[:, 0:1], M["a_proj0"], V["a_vb0"], start=True, stop=False)
                nc.tensor.matmul(ps[:, 0:1], M["a_proj1"], V["a_vb1"], start=False, stop=True).then_inc(product_made, 1)

            @block.vector
            def _(dve):
                nc.vector.memset(zero, 0.0).then_inc(setup_made, 1)
                dve.wait_ge(constants_loaded, 32)
                nc.vector.tensor_scalar(a_qb, V["a_qb"], head_scale, None, ALU.mult).then_inc(setup_made, 1)
                for dst, src in zip(halves + [half_b1], (V["c_s1b"], V["c_s2b"], V["c_s3b"], V["c_ff_b1"])):
                    nc.vector.tensor_scalar(dst, src, 0.5, None, ALU.mult).then_inc(setup_made, 1)
                dve.wait_ge(product_made, 1)
                nc.vector.tensor_tensor(a_out, ps[:, 0:1], V["a_pb"], ALU.add).then_inc(setup_made, 1)
                dve.wait_ge(setup_made, 7)

        with nc.cleanup_on_exit():
            attention(
                nc, "a", Plan([Group("S", 4, 0, 32), Group("S", 4, 4, 32)], True, "swwswpwswwswpw"), shared,
                {"qk": [M["a_q"], M["a_k"]], "v": M["a_v"], "proj": [M["a_proj0"], M["a_proj1"]]},
                x, None, x, scratch["y0"], scratch["parts"], head_scale,
                {"qk": [a_qb, V["a_kb"]], "out": a_out}, "bias")
        with ExitStack() as inner:
            sb = lambda name, shape: inner.enter_context(nc.sbuf_tensor(name, shape, F32))
            covs = [sb("cov_content", [P, P])[:, :], sb("cov_style", [P, P])[:, :]]
            move = sb("move", [P, P])[:, :]
            with nc.cleanup_on_exit():
                statistics(nc, "s", shared, style, STYLES, mean[1], covs[1])
            with nc.cleanup_on_exit():
                statistics(nc, "b", shared, scratch["y0"], NB, mean[0], covs[0])
            with nc.cleanup_on_exit():
                whiten(nc, M, shared, mean, covs, move, offset)
            with nc.cleanup_on_exit():
                gate(nc, M, V, shared, halves + [V["c_s2b"]], move, offset, scratch["y0"], pos,
                     scratch["h"], scratch["sh"], scratch["se"])
        with nc.cleanup_on_exit():
            attention(
                nc, "c", Plan([Group("S", 4, 0, 32), Group("S", 4, 4, 32), Group("D", 2, 0, 64)], True, "swwswwpswwswwp"), shared,
                {"qk": [M["c_q"], M["c_k"]], "v": M["c_v"], "dqk": [[M["c_dq0"], M["c_dq1"]], [M["c_dk0"], M["c_dk1"]]],
                 "vd": M["c_vd"], "proj": [M["c_ff0"], M["c_ff1"], M["c_ff2"]]},
                scratch["sh"], scratch["se"], None, scratch["ff"], scratch["parts"], float(HD) ** -0.5,
                {"qk": [0.0, 0.0], "dqk": [0.0, 0.0], "dscale": 0.5 * 64.0 ** -0.5}, "plain")
        with nc.cleanup_on_exit():
            feed_forward(nc, M, V, shared, half_b1, scratch["ff"], scratch["h"], scratch["z"])
        with nc.cleanup_on_exit():
            attention(
                nc, "d", Plan([Group("S", 1, 0, P)], False, "swwswpwswwswpw"), shared,
                {"qk": [M["d_qk"]], "vd": M["d_v"]},
                scratch["z"], None, scratch["z"], out, scratch["parts"], 1.0,
                {"qk": [V["d_qkb"]], "v": V["d_vb"], "gamma": V["d_gamma"]}, "gamma")


def kernel(**inputs):
    import concourse.bacc as _bacc
    from concourse.bass_utils import run_bass_kernel_spmd as _run

    i = {name: np.asarray(a) for name, a in inputs.items()}
    mats, mats_at = packed(matrices(i))
    vecs, vecs_at = packed(vectors(i))
    arrays = {
        "in_x": np.ascontiguousarray(i["x"]).reshape(NB, P, N),
        "in_style": np.ascontiguousarray(i["L1_conv_s_B"]).reshape(STYLES, P, N),
        "in_pos": np.ascontiguousarray(i["L2_conv_pos_emb"]).reshape(P, N),
        "in_mats": mats, "in_vecs": vecs,
    }
    nc = _bacc.Bacc("TRN2", target_bir_lowering=False, num_devices=1)
    given = [nc.dram_tensor(n, a.shape, F32, kind="ExternalInput").ap() for n, a in arrays.items()]
    out = nc.dram_tensor("out_image", (NB, P, N), F32, kind="ExternalOutput").ap()
    between = lambda name, shape, dt: nc.dram_tensor(name, shape, dt, kind="Internal").ap()
    scratch = {name: between(name, (NB, P, N), F32) for name in ("y0", "h", "sh", "se", "ff", "z")}
    scratch["parts"] = [between(name, (3, P, N), BF16) for name in ("q_parts", "k_parts")]
    program(nc, *given, mats_at, vecs_at, out, scratch)
    r = _run(nc, [arrays], core_ids=[0])
    return r.results[0]["out_image"].reshape(NB, P, SIDE, SIDE)
```
